# Optimizing a Trainium2 kernel written in Bass

```python
import numpy as np
import jax
import jax.numpy as jnp

def _softmax(x, axis=-1):
    return jax.nn.softmax(x, axis=axis)

def _gelu(x):
    return jax.nn.gelu(x, approximate=True)

def _silu(x):
    return jax.nn.silu(x)

def _sigmoid(x):
    return jax.nn.sigmoid(x)

def _layernorm(x, axis=-1, eps=1e-05):
    m = jnp.mean(x, axis=axis, keepdims=True)
    v = jnp.var(x, axis=axis, keepdims=True)
    return (x - m) / jnp.sqrt(v + eps)

def _scatter_add(tgt, idx, src, axis=0):
    return tgt.at[idx].add(src)

def _segment_sum(src, seg, n):
    return jax.ops.segment_sum(src, seg, n)
kernel_name = 'mk_decoder_postln_d1_seqx_r4_997548'

def setup_inputs(seed: int=0):
    np.random.seed(seed)
    _w = jnp.asarray

    def _rec_inputs():
        import jax
        import jax.numpy as jnp
        _rk = jax.random.key(seed)
        x = -0.000125 + 0.9999 * jax.random.normal(jax.random.fold_in(_rk, 1), (8, 112, 512), jnp.float32)
        _lenS = 112 - jax.random.randint(jax.random.fold_in(_rk, 7), (8,), 0, max(1, 112 // 4) + 1, jnp.int32)
        _lenS2 = 375 - jax.random.randint(jax.random.fold_in(_rk, 8), (8,), 0, max(1, 375 // 4) + 1, jnp.int32)
        _ctx_2048P = jax.random.normal(jax.random.fold_in(_rk, 11), (8, 16, 512), jnp.float32)
        _ctx_2048c = jax.random.dirichlet(jax.random.fold_in(_rk, 511), 0.3 * jnp.ones((16,), jnp.float32), (8, 375))
        _ctx_2048t = jnp.einsum('bsk,bkd->bsd', _ctx_2048c, _ctx_2048P)
        _ctx_2048t = _ctx_2048t * jax.lax.rsqrt(jnp.mean(jnp.square(_ctx_2048t)) + 1e-12) * 0.953939
        ctx_2048 = -1.52775e-05 + 0.999936 * (_ctx_2048t + 0.3 * jax.random.normal(jax.random.fold_in(_rk, 611), (8, 375, 512), jnp.float32))
        return (x, ctx_2048)
    x, ctx_2048 = _rec_inputs()

    def _L0_attn_setup():
        import jax, jax.numpy as jnp
        import numpy as np
        import math
        D_MODEL = 512
        N_HEADS = 16
        D_HEAD = 128
        BATCH = 2
        SEQ = 512
        key = jax.random.key(seed)
        ks = jax.random.split(key, 5)
        std = 0.02
        x = jax.random.normal(ks[0], (BATCH, SEQ, D_MODEL), dtype=jnp.float32)
        W_Q = std * jax.random.normal(ks[1], (N_HEADS, D_HEAD, D_MODEL), dtype=jnp.float32)
        W_K = std * jax.random.normal(ks[2], (N_HEADS, D_HEAD, D_MODEL), dtype=jnp.float32)
        W_V = std * jax.random.normal(ks[3], (N_HEADS, D_HEAD, D_MODEL), dtype=jnp.float32)
        W_O = std * jax.random.normal(ks[4], (N_HEADS, D_MODEL, D_HEAD), dtype=jnp.float32)
        return {'x': x, 'W_Q': W_Q, 'W_K': W_K, 'W_V': W_V, 'W_O': W_O}
    _L0_attn_all = _L0_attn_setup()
    _L0_attn_in = {k: v for k, v in _L0_attn_all.items() if k in ('W_Q', 'W_K', 'W_V', 'W_O')}
    del _L0_attn_all

    def _L0_xattn_setup():
        import jax, jax.numpy as jnp
        import numpy as np
        EPS = 1e-06
        NUM_HEADS = 16

        def _feature_map(x):
            return jnp.where(x > 0, x + 1.0, jnp.exp(x))
        key = jax.random.key(seed)
        ks = jax.random.split(key, 7)
        B, L, S, D = (4, 1024, 1024, 512)
        sc = 1.0 / np.sqrt(D)
        return {'query': jax.random.normal(ks[0], (B, L, D), jnp.float32), 'kv': jax.random.normal(ks[1], (B, S, D), jnp.float32), 'Wq': jax.random.normal(ks[2], (D, D), jnp.float32) * sc, 'Wg': jax.random.normal(ks[3], (D, D), jnp.float32) * sc, 'bg': jnp.ones((D,), jnp.float32), 'Wkv': jax.random.normal(ks[4], (2 * D, D), jnp.float32) * sc, 'Wo': jax.random.normal(ks[5], (D, D), jnp.float32) * sc}
    _L0_xattn_all = _L0_xattn_setup()
    _L0_xattn_in = {k: v for k, v in _L0_xattn_all.items() if k in ('Wq', 'Wg', 'bg', 'Wkv', 'Wo')}
    del _L0_xattn_all

    def _L0_ffn_setup():
        import jax, jax.numpy as jnp
        import numpy as np
        ALPHA = 1.702
        LIMIT = 7.0
        TOP_K = 2
        E, H, I = (8, 512, 512)
        B, S = (2, 512)
        key = jax.random.key(seed)
        ks = jax.random.split(key, 7)
        return {'hidden_states': jax.random.normal(ks[0], (B, S, H), dtype=jnp.float32), 'router_weight': jax.random.normal(ks[1], (E, H), dtype=jnp.float32) * 0.02, 'router_bias': jax.random.normal(ks[2], (E,), dtype=jnp.float32) * 0.02, 'gate_up_proj': jax.random.normal(ks[3], (E, H, 2 * I), dtype=jnp.float32) * 0.02, 'gate_up_proj_bias': jax.random.normal(ks[4], (E, 2 * I), dtype=jnp.float32) * 0.02, 'down_proj': jax.random.normal(ks[5], (E, I, H), dtype=jnp.float32) * 0.02, 'down_proj_bias': jax.random.normal(ks[6], (E, H), dtype=jnp.float32) * 0.02}
    _L0_ffn_all = _L0_ffn_setup()
    _L0_ffn_in = {k: v for k, v in _L0_ffn_all.items() if k in ('router_weight', 'router_bias', 'gate_up_proj', 'gate_up_proj_bias', 'down_proj', 'down_proj_bias')}
    del _L0_ffn_all
    return {'x': x, 'ctx_2048': ctx_2048, 'L0_attn_W_Q': _L0_attn_in['W_Q'], 'L0_attn_W_K': _L0_attn_in['W_K'], 'L0_attn_W_V': _L0_attn_in['W_V'], 'L0_attn_W_O': _L0_attn_in['W_O'], 'L0_xattn_Wq': _L0_xattn_in['Wq'], 'L0_xattn_Wg': _L0_xattn_in['Wg'], 'L0_xattn_bg': _L0_xattn_in['bg'], 'L0_xattn_Wkv': _L0_xattn_in['Wkv'], 'L0_xattn_Wo': _L0_xattn_in['Wo'], 'L0_ffn_router_weight': _L0_ffn_in['router_weight'], 'L0_ffn_router_bias': _L0_ffn_in['router_bias'], 'L0_ffn_gate_up_proj': _L0_ffn_in['gate_up_proj'], 'L0_ffn_gate_up_proj_bias': _L0_ffn_in['gate_up_proj_bias'], 'L0_ffn_down_proj': _L0_ffn_in['down_proj'], 'L0_ffn_down_proj_bias': _L0_ffn_in['down_proj_bias']}

def reference(x, ctx_2048, L0_attn_W_Q, L0_attn_W_K, L0_attn_W_V, L0_attn_W_O, L0_xattn_Wq, L0_xattn_Wg, L0_xattn_bg, L0_xattn_Wkv, L0_xattn_Wo, L0_ffn_router_weight, L0_ffn_router_bias, L0_ffn_gate_up_proj, L0_ffn_gate_up_proj_bias, L0_ffn_down_proj, L0_ffn_down_proj_bias):
    import jax
    import jax.numpy as jnp

    def _L0_attn_ref(x, W_Q, W_K, W_V, W_O):
        import jax, jax.numpy as jnp
        import numpy as np
        import math
        D_MODEL = 512
        N_HEADS = 16
        D_HEAD = 128
        BATCH = 2
        SEQ = 512
        d_head = W_Q.shape[1]
        seq_len = x.shape[1]
        scale = 1.0 / math.sqrt(d_head)
        q = jnp.einsum('bsd,hed->bhse', x, W_Q)
        k = jnp.einsum('bsd,hed->bhse', x, W_K)
        v = jnp.einsum('bsd,hed->bhse', x, W_V)
        scores = jnp.einsum('bhse,bhme->bhsm', q, k) * scale
        causal = jnp.triu(jnp.ones((seq_len, seq_len), dtype=bool), k=1)
        scores = jnp.where(causal, jnp.float32(-1000000000.0), scores)
        pattern = jax.nn.softmax(scores, axis=-1)
        z = jnp.einsum('bhsm,bhme->bhse', pattern, v)
        out = jnp.einsum('bhse,hde->bsd', z, W_O)
        return out

    def _L0_xattn_ref(query, kv, Wq, Wg, bg, Wkv, Wo):
        import jax, jax.numpy as jnp
        import numpy as np
        EPS = 1e-06
        NUM_HEADS = 16

        def _feature_map(x):
            return jnp.where(x > 0, x + 1.0, jnp.exp(x))
        B, L, D = query.shape
        S = kv.shape[1]
        H = NUM_HEADS
        hd = D // H
        q = query @ Wq.T
        gate = jax.nn.sigmoid(query @ Wg.T + bg)
        kvp = kv @ Wkv.T
        k, v = jnp.split(kvp, 2, axis=-1)
        q = _feature_map(q.reshape(B, L, H, hd).transpose(0, 2, 1, 3))
        k = _feature_map(k.reshape(B, S, H, hd).transpose(0, 2, 1, 3))
        v = v.reshape(B, S, H, hd).transpose(0, 2, 1, 3)
        kv_summary = jnp.einsum('bhsd,bhse->bhde', k, v)
        k_sum = k.sum(axis=-2)
        z = 1.0 / (jnp.einsum('bhld,bhd->bhl', q, k_sum)[..., None] + EPS)
        attn = jnp.einsum('bhld,bhde->bhle', q, kv_summary) * z
        attn = attn.transpose(0, 2, 1, 3).reshape(B, L, D)
        out = attn * gate @ Wo.T
        return out

    def _L0_ffn_ref(hidden_states, router_weight, router_bias, gate_up_proj, gate_up_proj_bias, down_proj, down_proj_bias):
        import jax, jax.numpy as jnp
        import numpy as np
        ALPHA = 1.702
        LIMIT = 7.0
        TOP_K = 2
        E, H, I = (8, 512, 512)
        B, S = (2, 512)
        bsz, seq_len, hidden = hidden_states.shape
        h = hidden_states.reshape(-1, hidden)
        T = h.shape[0]
        logits = h @ router_weight.T + router_bias
        top_vals, top_idx = jax.lax.top_k(logits, TOP_K)
        top_w = jax.nn.softmax(top_vals, axis=-1)
        scores = jnp.zeros_like(logits).at[jnp.arange(T)[:, None], top_idx].set(top_w)
        gate_up = jnp.einsum('th,ehj->etj', h, gate_up_proj) + gate_up_proj_bias[:, None, :]
        gate = gate_up[..., ::2]
        up = gate_up[..., 1::2]
        gate = jnp.minimum(gate, LIMIT)
        up = jnp.clip(up, -LIMIT, LIMIT)
        glu = gate * jax.nn.sigmoid(gate * ALPHA)
        act = (up + 1.0) * glu
        expert_out = jnp.einsum('eti,eih->eth', act, down_proj) + down_proj_bias[:, None, :]
        out = jnp.einsum('te,eth->th', scores, expert_out)
        return out.reshape(bsz, seq_len, hidden)
    x = _layernorm(x + _L0_attn_ref(x, L0_attn_W_Q, L0_attn_W_K, L0_attn_W_V, L0_attn_W_O), axis=-1)
    x = _layernorm(x + _L0_xattn_ref(x, ctx_2048, L0_xattn_Wq, L0_xattn_Wg, L0_xattn_bg, L0_xattn_Wkv, L0_xattn_Wo), axis=-1)
    x = _layernorm(x + _L0_ffn_ref(x, L0_ffn_router_weight, L0_ffn_router_bias, L0_ffn_gate_up_proj, L0_ffn_gate_up_proj_bias, L0_ffn_down_proj, L0_ffn_down_proj_bias), axis=-1)
    return x

_drawn_inputs = setup_inputs


def setup_inputs(seed=0):
    import zlib

    import numpy as np

    out = dict(_drawn_inputs(seed))
    spreads = {'L0_xattn_bg': (1.0, 0.6)}
    factors = {'L0_attn_W_Q': 3.122,
     'L0_attn_W_K': 2.884,
     'L0_xattn_Wq': 4.612,
     'L0_ffn_router_bias': 3.991,
     'L0_ffn_gate_up_proj_bias': 8.0,
     'L0_ffn_down_proj_bias': 3.973}
    for name, (base, spread) in spreads.items():
        noise = np.random.default_rng([zlib.crc32(name.encode()), seed]).standard_normal(out[name].shape)
        drawn = base * np.exp(spread * noise) if base else spread * noise
        out[name] = jnp.asarray(drawn.astype(out[name].dtype))
    for name, factor in factors.items():
        out[name] = (out[name] * factor).astype(out[name].dtype)
    return out
```

```python
from contextlib import ExitStack

import concourse.bass as bass
from concourse import mybir

ALU = mybir.AluOpType
ACT = mybir.ActivationFunctionType
AX = mybir.AxisListType
F32 = mybir.dt.float32
F32R = mybir.dt.float32r
U32 = mybir.dt.uint32

P = 128
LN_EPS, DEN_EPS = 1e-5, 1e-6
ALPHA, LIMIT = 1.702, 7.0
NEG = -1e9


def decoder_layer(nc: bass.Bass, t: dict, out: bass.AP):
    NB, S, D = t["x"].shape
    T = NB * S
    KC = D // P
    NP_ = t["w_qkv"].shape[0]
    E = P
    HALF = T // 2
    NT = T // P
    SC = t["ctx_t"].shape[3]
    CT = 3
    CM = SC // CT
    NE = t["w_gu"].shape[0]
    FI = t["w_down"].shape[2] * 1
    BH = NB // 2
    SCALE = float(E) ** -0.5
    NCT = NB * CT
    TOK0 = [0, 4 * P]
    TOKN = [4 * P, T - 4 * P]

    with ExitStack() as ctx:
        def sb(name, shape, dt=F32):
            return ctx.enter_context(nc.sbuf_tensor(name, shape, dt))

        def sem(name):
            return ctx.enter_context(nc.semaphore(name))

        R = sb("R", [P, 31744], F32R)
        F = sb("F", [P, 20096])
        ident = sb("ident", [P, P])
        causal = sb("causal", [P, S])
        blocks = sb("blocks", [P, P])
        iota = sb("iota", [P, NE])
        ones = sb("ones", [P, 2])
        neg_max = sb("neg_max", [P, 16])
        exp_sum = sb("exp_sum", [P, 16])
        exp_inv = sb("exp_inv", [P, 16])
        ln_st = sb("ln_st", [P, NT, 6])
        ln_mv = sb("ln_mv", [P, NT, 2])
        ln_ve = sb("ln_ve", [P, NT])
        ln_sd = sb("ln_sd", [P, NT])
        ln_rs = sb("ln_rs", [P, NT])
        k_sum = sb("k_sum", [P, NB, KC])
        gate_b = sb("gate_b", [P, KC])
        rt_w = sb("rt_w", [P, KC, NE])
        rt_hi = sb("rt_hi", [P, KC, NE], F32R)
        rt_lo = sb("rt_lo", [P, KC, NE], F32R)
        rt_b = sb("rt_b", [P, NE])
        logit = sb("logit", [P, NT, NE])
        top = sb("top", [P, NT, 8])
        top_i = sb("top_i", [P, NT, 8], U32)
        top_f = sb("top_f", [P, NT, 2])
        top_d = sb("top_d", [P, NT, 2])
        top_w = sb("top_w", [P, NT, 2])
        pick = sb("pick", [P, 2, NE])
        score = sb("score", [P, NT, NE])
        gu_b = sb("gu_b", [P, NE, 2 * KC])
        banks = [ctx.enter_context(nc.psum_tensor(f"bank{i}", [P, 512], F32)) for i in range(8)]

        def r(at, shape):
            n = 1
            for s in shape:
                n *= s
            v = R[:, at:at + 2 * n]
            if len(shape) == 1:
                return v.rearrange("p (o a) -> p o a", o=2)
            return v.rearrange("p (o a b) -> p o a b", o=2, a=shape[0])

        def f(at, *shape):
            n = 1
            for s in shape:
                n *= s
            v = F[:, at:at + n]
            if len(shape) == 1:
                return v
            if len(shape) == 2:
                return v.rearrange("p (a b) -> p a b", a=shape[0])
            return v.rearrange("p (a b c) -> p a b c", a=shape[0], b=shape[1])

        def bits(ap):
            return ap.bitcast(F32)

        xT = r(0, (KC, T))
        w_qkv = [[r(7168 + 6144 * s + 2048 * j, (KC, 2 * E)) for j in range(3)] for s in range(2)]
        zT = r(19456, (2, T))
        w_o = r(23040, (2, D))
        w_kv = r(7168, (KC, 2 * D))
        cT = [r(15360, (KC, SC)), r(19456, (KC, SC))]
        w_q = r(22500, (KC, D))
        w_g = r(26596, (KC, D))
        w_xo = r(7168, (KC, D))
        aT = r(23552, (KC, T))
        w_gu = [r(15360, (KC, 2 * D)), r(7168, (KC, 2 * D))]
        w_dn = r(23552, (KC, D))
        hT = r(27648, (KC, 512))
        raw_w = f(0, 3, KC, 2 * E)
        raw_o = f(3072, 2, D)
        acc = f(4096, NT, D)
        qT = f(7680, 2, T)
        kT = f(9472, 2, T)
        prob = f(11264, 4, BH, S)
        probT = f(13056, 2, BH, S)
        V = f(13952, 2, NB, 2 * E)
        raw_x = f(13952, KC, T)
        raw_kv = [f(0, 2, 2 * D), f(18048, 2, 2 * D)]
        raw_c = [f(0, KC, SC), f(1500, KC, SC)]
        phi_k = f(7680, 3, D)
        v_c = f(9216, 3, D)
        relu_c = f(10752, 2, D)
        exp_c = f(11776, 2, D)
        kv_sum = f(13952, NB, KC, P)
        raw_x3 = f(18048, KC, D)
        phi_q = f(7680, KC, T)
        relu_q = f(11264, 2, HALF)
        exp_q = f(12160, 2, HALF)
        sig = f(0, KC, T)
        k_blk = f(11264, 2, KC, P)
        atn = f(12288, 2, KC, S)
        raw_gu = f(0, KC, 2 * D)
        gl = f(7680, 2, 512)
        sg = f(8704, 2, 512)
        up = f(9728, 2, 512)
        pr = f(10752, 2, 512)
        hh = f(11776, 2, 512)
        dn_b = f(12800, D)
        scoreT = f(13312, T)

        in_const = sem("in_const")
        in_x = [sem(f"in_xt{k}") for k in range(KC)]
        in_acc = sem("in_acc")
        in_w = [sem(f"in_w{j}") for j in range(3)]
        in_wo = sem("in_wo")
        in_kv = [sem(f"in_kv{j}") for j in range(2)]
        in_c = [sem(f"in_c{j}") for j in range(2)]
        in_x3 = sem("in_x3")
        in_gu = sem("in_gu")
        in_dnb = sem("in_dnb")
        out_done = sem("out_done")
        names = """ones_set x_hi x_lo w_hi w_lo wo_hi wo_lo q_mm v_mm qk_out v_out s_mm masked neg_max_ok exp_ok inv_ok
            prob_ok pt_mm pt_out z_mm z_hi z_lo o_mm o_add kv_hi kv_lo c_hi c_lo ck_mm cv_mm ck_relu ck_exp
            phi_ok cv_out sum_mm sum_out bn_ok mv_ok ve_ok sd_ok rs_ok ln_ok t_mm t_hi t_lo
            x3_hi x3_lo q2_mm q2_act q2_phi g2_mm g2_sig blk_ok a_mm a_den a_inv a_num a_gate a_hi a_lo xo_mm xo_add
            rt_ok r_mm log_ok top_ok idx_ok topf_ok topd_ok topw_ok pick_ok score_ok st_mm st_out db_mm db_add
            gub_ok gu_hi gu_lo gu_mm gl_ok up_ok sg_ok pr_ok hh_ok h_hi h_lo dn_mm dn_add""".split()
        m = {n: sem(n) for n in names}

        block = ctx.enter_context(nc.Block())

        PASSES = ((0, 0), (0, 1), (1, 0))

        def products(mm_out, lhs, rhs, n):
            for k in range(n):
                for i, (a, b) in enumerate(PASSES):
                    last = nc.tensor.matmul(mm_out, lhs(a, k), rhs(b, k), start=(k == 0 and i == 0),
                                            stop=(k == n - 1 and i == 2))
            return last

        @block.sync
        def _(sp):
            for k in range(KC):
                sp.dma_start(raw_x[:, k, :], t["x_t"][:, k, :]).then_inc(in_x[k], 16)
                if k < 3:
                    sp.dma_start(raw_w[:, k], t["w_qkv"][0, :, k]).then_inc(in_w[k], 16)
            for dst, src in ((ident, "ident"), (causal, "causal"), (blocks, "blocks"), (iota, "iota"),
                             (gate_b, "gate_b"), (rt_b, "rt_b")):
                sp.dma_start(dst[:, :], t[src]).then_inc(in_const, 16)
            sp.dma_start(rt_w[:, :, :], t["rt_w"]).then_inc(in_const, 16)
            sp.dma_start(gu_b[:, :, :], t["gu_b"]).then_inc(in_const, 16)
            sp.dma_start(raw_o, t["w_o"][0]).then_inc(in_wo, 16)
            sp.dma_start(acc, t["x"].rearrange("b s d -> (b s) d").rearrange("(n p) d -> p n d", p=P)).then_inc(in_acc, 16)
            for p in range(1, NP_):
                for j in range(3):
                    sp.wait_ge(m["w_lo"], 3 * (p - 1) + j + 1)
                    sp.dma_start(raw_w[:, j], t["w_qkv"][p, :, j]).then_inc(in_w[j], 16)
                if p >= 1:
                    sp.wait_ge(m["wo_lo"], p)
                    sp.dma_start(raw_o, t["w_o"][p]).then_inc(in_wo, 16)
            sp.wait_ge(m["w_lo"], 3 * NP_)
            sp.dma_start(raw_kv[0], t["w_kv"][:, 0:2]).then_inc(in_kv[0], 16)
            sp.dma_start(raw_kv[1], t["w_kv"][:, 2:4]).then_inc(in_kv[1], 16)
            sp.wait_ge(m["kv_lo"], KC)
            sp.dma_start(raw_x3, t["w_x3"][0]).then_inc(in_x3, 16)
            for b in range(NB):
                if b >= 2:
                    sp.wait_ge(m["c_lo"], b - 1)
                sp.dma_start(raw_c[b % 2], t["ctx_t"][b]).then_inc(in_c[b % 2], 16)
                if b in (3, 5):
                    j = (b - 1) // 2
                    sp.wait_ge(m["x3_lo"], j)
                    sp.dma_start(raw_x3, t["w_x3"][j]).then_inc(in_x3, 16)
            for e in range(NE):
                if e == 0:
                    sp.wait_ge(m["a_gate"], NB)
                    sp.wait_ge(m["x3_lo"], 3)
                else:
                    sp.wait_ge(m["gu_lo"], KC * e)
                sp.dma_start(raw_gu, t["w_gu"][e]).then_inc(in_gu, 16)
                if e > 0:
                    sp.wait_ge(m["x3_lo"], 3 + e)
                sp.dma_start(raw_x3, t["w_down"][e]).then_inc(in_x3, 16)
                if e == 0:
                    sp.wait_ge(m["a_lo"], NB)
                    sp.dma_start(dn_b[0:NE, :], t["dn_b"]).then_inc(in_dnb, 16)
            o = out.rearrange("b s d -> (b s) d").rearrange("(n p) d -> p n d", p=P)
            for n in range(NT):
                sp.wait_ge(m["ln_ok"], 2 * NT + n + 1)
                sp.dma_start(o[:, n, :], acc[:, n, :]).then_inc(out_done, 16)
            sp.wait_ge(out_done, 16 * NT)

        @block.gpsimd
        def _(pool):
            nc.gpsimd.memset(ones[:, :], 1.0).then_inc(m["ones_set"], 1)
            pool.wait_ge(m["q2_phi"], 2 * KC)
            for b in range(NB):
                if b >= 2:
                    pool.wait_ge(m["a_mm"], b - 1)
                pool.wait_ge(m["sum_out"], 2 * (b + 1))
                nc.gpsimd.tensor_tensor(k_blk[:, b % 2], blocks[:, :].unsqueeze(1).to_broadcast([P, KC, P]),
                                        k_sum[:, b, :].unsqueeze(2).to_broadcast([P, KC, P]),
                                        ALU.mult).then_inc(m["blk_ok"], 1)
            n = 0
            for e in range(NE):
                for hf in range(2):
                    N = TOKN[hf]
                    for c in range(KC):
                        pool.wait_ge(m["sg_ok"], n + 1)
                        if n >= 2:
                            pool.wait_ge(m["hh_ok"], n - 1)
                        nc.gpsimd.tensor_tensor(pr[:, n % 2, 0:N], gl[:, n % 2, 0:N], sg[:, n % 2, 0:N],
                                                ALU.mult).then_inc(m["pr_ok"], 1)
                        n += 1

        @block.tensor
        def _(pe):
            def scores(p):
                pe.wait_ge(m["qk_out"], 8 * (p + 1))
                for g in range(4):
                    h, hf, n = g // 2, g % 2, 4 * p + g
                    if n >= 2:
                        pe.wait_ge(m["masked"], n - 1)
                    for j in range(BH):
                        c = (hf * BH + j) * S
                        mm = nc.tensor.matmul(banks[2 + g % 2][0:S, j * S:(j + 1) * S], qT[:, h, c:c + S],
                                              kT[:, h, c:c + S], start=True, stop=True)
                    mm.then_inc(m["s_mm"], 1)

            def out_proj(p):
                pe.wait_ge(m["z_lo"], 4 * (p + 1))
                pe.wait_ge(m["wo_lo"], p + 1)
                for n in range(NT):
                    if n == 0:
                        pe.wait_ge(m["v_out"], 4 * min(p + 2, NP_))
                    if n >= 2:
                        pe.wait_ge(m["o_add"], NT * p + n - 1)
                    products(banks[n % 2][:, :], lambda a, k: zT[:, a, k, n * P:(n + 1) * P],
                             lambda b, k: w_o[:, b, k, :], 2).then_inc(m["o_mm"], 1)

            def proj(p):
                w = w_qkv[p % 2]
                for j in range(8):
                    part, h, hf = j // 4, (j // 2) % 2, j % 2
                    if p == 0 and j == 0:
                        pe.wait_ge(m["x_lo"], KC)
                    if j % 4 == 0:
                        pe.wait_ge(m["w_lo"], 3 * p + part + 1)
                    if j < 2 and p >= 2:
                        pe.wait_ge(m["o_add"], NT * (p - 2) + NT - 1 + j)
                    if j < 2 and p == 1:
                        pe.wait_ge(m["v_out"], 4)
                    if j >= 2:
                        pe.wait_ge(m["qk_out"], 8 * p + j - 1)
                    products(banks[(1 + j) % 2][:, 0:HALF], lambda a, k: w[part][:, a, k, h * E:(h + 1) * E],
                             lambda b, k: xT[:, b, k, hf * HALF:(hf + 1) * HALF], KC).then_inc(m["q_mm"], 1)
                pe.wait_ge(m["w_lo"], 3 * p + 3)
                for j in range(4):
                    if j < 2:
                        pe.wait_ge(m["qk_out"], 8 * p + 7 + j)
                    else:
                        pe.wait_ge(m["v_out"], 4 * p + j - 1)
                    for i in range(2):
                        b0 = (2 * j + i) * S
                        mm = products(banks[(1 + j) % 2][0:S, i * 256:(i + 1) * 256],
                                      lambda a, k: xT[:, a, k, b0:b0 + S], lambda b, k: w[2][:, b, k, :], KC)
                    mm.then_inc(m["v_mm"], 1)

            def attend(p):
                def turn(g):
                    n = 4 * p + g
                    pe.wait_ge(m["prob_ok"], n + 1)
                    if n >= 2:
                        pe.wait_ge(m["pt_out"], n - 1)
                    for j in range(BH):
                        mm = nc.tensor.transpose(banks[4 + g % 2][0:S, j * S:(j + 1) * S], prob[0:S, g, j, :],
                                                 ident[0:S, 0:S])
                    mm.then_inc(m["pt_mm"], 1)

                def values(g):
                    n, h, hf = 4 * p + g, g // 2, g % 2
                    pe.wait_ge(m["pt_out"], n + 1)
                    if n >= 2:
                        pe.wait_ge(m["z_lo"], n - 1)
                    for j in range(BH):
                        mm = nc.tensor.matmul(banks[6 + g % 2][:, j * S:(j + 1) * S],
                                              V[0:S, p % 2, hf * BH + j, h * E:(h + 1) * E],
                                              probT[0:S, g % 2, j, :], start=True, stop=True)
                    mm.then_inc(m["z_mm"], 1)

                pe.wait_ge(m["v_out"], 4 * (p + 1))
                turn(0)
                turn(1)
                values(0)
                turn(2)
                values(1)
                turn(3)
                values(2)
                values(3)

            def turn_acc(n, bank, ln, t_first, prev):
                pe.wait_ge(m["ln_ok"], NT * ln + n + 1)
                if prev:
                    pe.wait_ge(m["t_lo"], prev)
                for k in range(KC):
                    mm = nc.tensor.transpose(banks[bank][:, k * P:(k + 1) * P], acc[:, n, k * P:(k + 1) * P],
                                             ident[:, :])
                mm.then_inc(m["t_mm"], 1)

            proj(0)
            pe.wait_ge(in_const, 16 * 8)
            for p in range(NP_):
                scores(p)
                if p >= 1:
                    out_proj(p - 1)
                if p + 1 < NP_:
                    proj(p + 1)
                attend(p)
            out_proj(NP_ - 1)

            def sums(n):
                b, c = n // CT, n % CT
                pe.wait_ge(m["phi_ok"], n + 1)
                pe.wait_ge(m["cv_out"], n + 1)
                if c == 0 and b >= 1:
                    pe.wait_ge(m["sum_out"], 2 * b)
                if n == 0:
                    pe.wait_ge(m["ones_set"], 1)
                for g in range(KC):
                    nc.tensor.matmul(banks[4 + b % 2][:, g * P:(g + 1) * P], phi_k[0:CM, n % 3, g * P:(g + 1) * P],
                                     v_c[0:CM, n % 3, g * P:(g + 1) * P], start=(c == 0 and g == 0),
                                     stop=(c == CT - 1), skip_group_check=True)
                    mm = nc.tensor.matmul(banks[6][:, g:g + 1], phi_k[0:CM, n % 3, g * P:(g + 1) * P],
                                          ones[0:CM, 0:1], start=(c == 0 and g == 0), stop=(c == CT - 1),
                                          skip_group_check=True)
                mm.then_inc(m["sum_mm"], 1)

            for n in range(NCT):
                b, c = n // CT, n % CT
                if c == 0:
                    pe.wait_ge(m["c_lo"], b + 1)
                if n == 0:
                    pe.wait_ge(m["kv_lo"], KC)
                    pe.wait_ge(m["o_add"], NT * NP_)
                if n >= 2:
                    pe.wait_ge(m["ck_exp"], n - 1)
                products(banks[n % 2][0:CM, :], lambda a, k: cT[b % 2][:, a, k, c * CM:(c + 1) * CM],
                         lambda q, k: w_kv[:, q, k, 0:D], KC).then_inc(m["ck_mm"], 1)
                if n >= 2:
                    pe.wait_ge(m["cv_out"], n - 1)
                products(banks[2 + n % 2][0:CM, :], lambda a, k: cT[b % 2][:, a, k, c * CM:(c + 1) * CM],
                         lambda q, k: w_kv[:, q, k, D:2 * D], KC).then_inc(m["cv_mm"], 1)
                if n >= 1:
                    sums(n - 1)
                if c == CT - 1 and b >= 1:
                    turn_acc(b - 1, 7, 0, 0, b - 1)
            sums(NCT - 1)

            pe.wait_ge(m["t_lo"], NT)
            pe.wait_ge(m["x3_lo"], 2)
            for n in range(4 * KC):
                j = n % (2 * KC)
                g, hf = j // 2, j % 2
                w = w_q if n < 2 * KC else w_g
                if n < 2:
                    pe.wait_ge(m["ck_exp"], NCT)
                elif n < 2 * KC + 2:
                    pe.wait_ge(m["q2_act"], n - 1)
                else:
                    pe.wait_ge(m["g2_sig"], n - 2 * KC - 1)
                products(banks[n % 2][:, 0:HALF], lambda a, k: w[:, a, k, g * P:(g + 1) * P],
                         lambda q, k: xT[:, q, k, hf * HALF:(hf + 1) * HALF], KC)\
                    .then_inc(m["q2_mm"] if n < 2 * KC else m["g2_mm"], 1)
            pe.wait_ge(m["q2_phi"], 2 * KC)
            pe.wait_ge(m["sum_out"], 2 * NB)
            for b in range(NB):
                pe.wait_ge(m["blk_ok"], b + 1)
                if b >= 2:
                    pe.wait_ge(m["a_num"], b - 1)
                for g in range(KC):
                    nc.tensor.matmul(banks[6 + b % 2][:, g * S:(g + 1) * S], k_blk[:, b % 2, g, :],
                                     phi_q[:, g, b * S:(b + 1) * S], start=True, stop=True)
                    mm = nc.tensor.matmul(banks[4 + b % 2][:, g * S:(g + 1) * S], kv_sum[:, b, g, :],
                                          phi_q[:, g, b * S:(b + 1) * S], start=True, stop=True)
                mm.then_inc(m["a_mm"], 1)
            pe.wait_ge(m["x3_lo"], 3)
            pe.wait_ge(m["cv_out"], NCT)
            for n in range(NT):
                pe.wait_ge(m["a_lo"], -(-(n + 1) * P // S))
                if n >= 2:
                    pe.wait_ge(m["xo_add"], n - 1)
                products(banks[2 + n % 2][:, :], lambda a, k: aT[:, a, k, n * P:(n + 1) * P],
                         lambda q, k: w_xo[:, q, k, :], KC).then_inc(m["xo_mm"], 1)
            pe.wait_ge(m["rt_ok"], 2)
            for n in range(NT):
                turn_acc(n, 4 + n % 2, 1, 0, NT + n - 1 if n >= 2 else 0)
                if n >= 1:
                    pe.wait_ge(m["t_lo"], NT + n)
                    products(banks[6][:, (n - 1) * NE:n * NE], lambda a, k: xT[:, a, k, (n - 1) * P:n * P],
                             lambda q, k: (rt_hi, rt_lo)[q][:, k, :], KC).then_inc(m["r_mm"], 1)
            n = NT
            pe.wait_ge(m["t_lo"], NT + n)
            products(banks[6][:, (n - 1) * NE:n * NE], lambda a, k: xT[:, a, k, (n - 1) * P:n * P],
                     lambda q, k: (rt_hi, rt_lo)[q][:, k, :], KC).then_inc(m["r_mm"], 1)
            pe.wait_ge(m["score_ok"], NT)
            pe.wait_ge(in_dnb, 16)
            for n in range(NT):
                mm = nc.tensor.transpose(banks[(0 if n < 4 else 1)][0:NE, (n % 4) * P:(n % 4 + 1) * P], score[:, n, :], ident[:, :])
            mm.then_inc(m["st_mm"], 1)
            pe.wait_ge(m["st_out"], 2)
            for n in range(NT):
                if n >= 2:
                    pe.wait_ge(m["db_add"], n - 1)
                nc.tensor.matmul(banks[2 + n % 2][:, :], scoreT[0:NE, n * P:(n + 1) * P], dn_b[0:NE, :],
                                 start=True, stop=True).then_inc(m["db_mm"], 1)

            def gate_up(n):
                e, hf, c = n // (2 * KC), (n // KC) % 2, n % KC
                t0, N = TOK0[hf], TOKN[hf]
                w = w_gu[e % 2]
                if hf == 0 and c == 0:
                    pe.wait_ge(m["gu_lo"], KC * (e + 1))
                if n >= 2:
                    pe.wait_ge(m["up_ok"], n - 1)
                if n == 0:
                    pe.wait_ge(m["db_add"], NT)
                products(banks[n % 2][:, 0:N], lambda a, k: w[:, a, k, c * P:(c + 1) * P],
                         lambda q, k: xT[:, q, k, t0:t0 + N], KC)
                products(banks[2 + n % 2][:, 0:N], lambda a, k: w[:, a, k, D + c * P:D + (c + 1) * P],
                         lambda q, k: xT[:, q, k, t0:t0 + N], KC).then_inc(m["gu_mm"], 1)

            def down(i):
                e, hf = i // 2, i % 2
                pe.wait_ge(m["x3_lo"], 3 + e + 1)
                pe.wait_ge(m["h_lo"], KC * (i + 1))
                for j in range(TOKN[hf] // P):
                    n = e * NT + 4 * hf + j
                    if n >= 4:
                        pe.wait_ge(m["dn_add"], n - 3)
                    products(banks[4 + n % 4][:, :], lambda a, k: hT[:, a, k, j * P:(j + 1) * P],
                             lambda q, k: w_dn[:, q, k, :], KC).then_inc(m["dn_mm"], 1)

            for i in range(2 * NE):
                for c in range(KC):
                    gate_up(KC * i + c)
                    if c == 1 and i >= 1:
                        down(i - 1)
            down(2 * NE - 1)

        @block.scalar
        def _(act):
            def split_hi(dst, src):
                return nc.scalar.copy(dst, src)

            def w_high(p, j):
                act.wait_ge(in_w[j], 16 * (p + 1))
                if p >= 2:
                    act.wait_ge(m["v_mm"], 4 * (p - 1))
                split_hi(w_qkv[p % 2][j][:, 0], raw_w[:, j]).then_inc(m["w_hi"], 1)

            def wo_high(p):
                act.wait_ge(in_wo, 16 * (p + 1))
                if p >= 1:
                    act.wait_ge(m["o_mm"], NT * p)
                split_hi(w_o[:, 0], raw_o).then_inc(m["wo_hi"], 1)

            def qk_evac(p, j):
                part, h, hf = j // 4, (j // 2) % 2, j % 2
                act.wait_ge(m["q_mm"], 8 * p + j + 1)
                if p >= 1:
                    act.wait_ge(m["s_mm"], 4 * p)
                dst = (qT, kT)[part]
                nc.scalar.copy(dst[:, h, hf * HALF:(hf + 1) * HALF], banks[(1 + j) % 2][:, 0:HALF])\
                    .then_inc(m["qk_out"], 1)

            for k in range(KC):
                act.wait_ge(in_x[k], 16)
                split_hi(xT[:, 0, k], raw_x[:, k]).then_inc(m["x_hi"], 1)
                if k < 3:
                    w_high(0, k)
            wo_high(0)
            for j in range(8):
                qk_evac(0, j)
                if j in (1, 3, 5):
                    w_high(1, j // 2)
            for p in range(NP_):
                for g in range(4):
                    act.wait_ge(m["neg_max_ok"], 4 * p + g + 1)
                    if g == 0 and p >= 1:
                        act.wait_ge(m["inv_ok"], p)
                    for j in range(BH):
                        i = g * BH + j
                        e = nc.scalar.activation(prob[0:S, g, j, :], prob[0:S, g, j, :], ACT.Exp,
                                                 bias=neg_max[0:S, i:i + 1], scale=-1.0,
                                                 accum_out=exp_sum[0:S, i:i + 1])
                    e.then_inc(m["exp_ok"], 1)
                if p >= 1:
                    wo_high(p)
                if p + 1 < NP_:
                    for j in range(8):
                        qk_evac(p + 1, j)
                        if j in (1, 3, 5) and p + 2 < NP_:
                            w_high(p + 2, j // 2)
                else:
                    act.wait_ge(m["v_mm"], 4 * NP_)
                    for k in range(KC):
                        act.wait_ge(in_kv[k // 2], 16)
                        split_hi(w_kv[:, 0, k], raw_kv[k // 2][:, k % 2]).then_inc(m["kv_hi"], 1)
                for g in range(4):
                    act.wait_ge(m["z_mm"], 4 * p + g + 1)
                    if p >= 1:
                        act.wait_ge(m["o_mm"], NT * p)
                    h, hf = g // 2, g % 2
                    nc.scalar.copy(zT[:, 0, h, hf * HALF:(hf + 1) * HALF], banks[6 + g % 2][:, 0:HALF])\
                        .then_inc(m["z_hi"], 1)

            def c_high(b):
                act.wait_ge(in_c[b % 2], 16 * (b // 2 + 1))
                if b >= 2:
                    act.wait_ge(m["cv_mm"], CT * (b - 1))
                if b == 1:
                    act.wait_ge(m["o_mm"], NT * NP_)
                split_hi(cT[b % 2][:, 0], raw_c[b % 2]).then_inc(m["c_hi"], 1)

            def std(ln):
                act.wait_ge(m["ve_ok"], ln + 1)
                nc.scalar.activation(ln_sd[:, :], ln_ve[:, :], ACT.Sqrt).then_inc(m["sd_ok"], 1)

            def turned_hi(n, i, bank):
                act.wait_ge(m["t_mm"], i + 1)
                nc.scalar.copy(xT[:, 0, :, n * P:(n + 1) * P],
                               banks[bank][:, :].rearrange("p (k c) -> p k c", k=KC)).then_inc(m["t_hi"], 1)

            def x3_high(j, dst):
                act.wait_ge(in_x3, 16 * (j + 1))
                split_hi(dst[:, 0], raw_x3).then_inc(m["x3_hi"], 1)

            c_high(0)
            c_high(1)
            for n in range(NCT):
                b, c = n // CT, n % CT
                act.wait_ge(m["ck_mm"], n + 1)
                if n >= 2:
                    act.wait_ge(m["phi_ok"], n - 1)
                nc.scalar.activation(relu_c[0:CM, n % 2, :], banks[n % 2][0:CM, :], ACT.Relu).then_inc(m["ck_relu"], 1)
                nc.scalar.activation(exp_c[0:CM, n % 2, :], banks[n % 2][0:CM, :], ACT.Exp).then_inc(m["ck_exp"], 1)
                if c == CT - 1:
                    if b == 0:
                        std(0)
                        act.wait_ge(in_const, 16 * 8)
                        split_hi(rt_hi[:, :, :], rt_w[:, :, :]).then_inc(m["rt_ok"], 1)
                    if b >= 1:
                        turned_hi(b - 1, b - 1, 7)
                    if b in (1, 3):
                        x3_high(b // 2, (w_q, w_g)[b // 2])
                    if b + 2 < NB:
                        c_high(b + 2)
            for j in range(2 * KC):
                act.wait_ge(m["q2_mm"], j + 1)
                if j >= 2:
                    act.wait_ge(m["q2_phi"], j - 1)
                else:
                    act.wait_ge(m["phi_ok"], NCT)
                nc.scalar.activation(relu_q[:, j % 2, :], banks[j % 2][:, 0:HALF], ACT.Relu)
                nc.scalar.activation(exp_q[:, j % 2, :], banks[j % 2][:, 0:HALF], ACT.Exp).then_inc(m["q2_act"], 1)
            x3_high(2, w_xo)
            act.wait_ge(m["c_lo"], NB)
            for j in range(2 * KC):
                g, hf = j // 2, j % 2
                act.wait_ge(m["g2_mm"], j + 1)
                nc.scalar.activation(sig[:, g, hf * HALF:(hf + 1) * HALF], banks[j % 2][:, 0:HALF], ACT.Sigmoid,
                                     bias=gate_b[:, g:g + 1]).then_inc(m["g2_sig"], 1)
            for b in range(NB):
                act.wait_ge(m["a_gate"], b + 1)
                split_hi(aT[:, 0, :, b * S:(b + 1) * S], atn[:, b % 2]).then_inc(m["a_hi"], 1)
            def gu_high(e):
                act.wait_ge(in_gu, 16 * (e + 1))
                if e >= 2:
                    act.wait_ge(m["gu_mm"], 2 * KC * (e - 1))
                if e == 1:
                    act.wait_ge(m["xo_mm"], NT)
                for k in range(KC):
                    split_hi(w_gu[e % 2][:, 0, k], raw_gu[:, k]).then_inc(m["gu_hi"], 1)

            gu_high(0)
            std(1)
            for n in range(NT):
                turned_hi(n, NT + n, 4 + n % 2)
            act.wait_ge(m["xo_mm"], NT)
            x3_high(3, w_dn)
            act.wait_ge(m["topd_ok"], NT)
            nc.scalar.activation(top_w[:, :, :], top_d[:, :, :], ACT.Sigmoid).then_inc(m["topw_ok"], 1)
            act.wait_ge(m["st_mm"], 1)
            nc.scalar.copy(scoreT[0:NE, 0:4 * P], banks[0][0:NE, :]).then_inc(m["st_out"], 1)
            nc.scalar.copy(scoreT[0:NE, 4 * P:T], banks[1][0:NE, 0:T - 4 * P]).then_inc(m["st_out"], 1)

            def h_high(n):
                i, c = n // KC, n % KC
                N = TOKN[i % 2]
                act.wait_ge(m["hh_ok"], n + 1)
                if i >= 1:
                    act.wait_ge(m["dn_mm"], NT * (i // 2) + 4 * (i % 2))
                nc.scalar.copy(hT[:, 0, c, 0:N], hh[:, n % 2, 0:N]).then_inc(m["h_hi"], 1)

            for n in range(2 * NE * KC):
                i, c = n // KC, n % KC
                N = TOKN[i % 2]
                act.wait_ge(m["gl_ok"], n + 1)
                if n >= 2:
                    act.wait_ge(m["pr_ok"], n - 1)
                nc.scalar.activation(sg[:, n % 2, 0:N], gl[:, n % 2, 0:N], ACT.Sigmoid, scale=ALPHA)\
                    .then_inc(m["sg_ok"], 1)
                if n >= 1:
                    h_high(n - 1)
                e = n // (2 * KC)
                if n % (2 * KC) == 1 and e + 1 < NE:
                    gu_high(e + 1)
                if n % (2 * KC) == 4 and e >= 1:
                    act.wait_ge(m["dn_mm"], NT * e)
                    x3_high(3 + e, w_dn)
            h_high(2 * NE * KC - 1)
            std(2)

        @block.vector
        def _(dve):
            def split_lo(dst, src, hi):
                return nc.vector.tensor_tensor(dst, src, bits(hi), ALU.subtract)

            def w_low(p, j):
                dve.wait_ge(m["w_hi"], 3 * p + j + 1)
                split_lo(w_qkv[p % 2][j][:, 1], raw_w[:, j], w_qkv[p % 2][j][:, 0]).then_inc(m["w_lo"], 1)

            def wo_low(p):
                dve.wait_ge(m["wo_hi"], p + 1)
                split_lo(w_o[:, 1], raw_o, w_o[:, 0]).then_inc(m["wo_lo"], 1)

            def v_evac(p):
                for j in range(4):
                    dve.wait_ge(m["v_mm"], 4 * p + j + 1)
                    if p == 0:
                        dve.wait_ge(m["x_lo"], KC)
                    if p >= 2:
                        dve.wait_ge(m["z_mm"], 4 * (p - 1))
                    nc.vector.tensor_copy(V[0:S, p % 2, 2 * j:2 * j + 2, :],
                                          banks[(1 + j) % 2][0:S, :].rearrange("p (a c) -> p a c", a=2))\
                        .then_inc(m["v_out"], 1)

            def add_out(p):
                for n in range(NT):
                    dve.wait_ge(m["o_mm"], NT * p + n + 1)
                    if p == 0 and n == 0:
                        dve.wait_ge(in_acc, 16)
                    if p >= 1:
                        dve.wait_ge(m["o_add"], NT * (p - 1) + n + 1)
                    nc.vector.tensor_tensor(acc[:, n, :], acc[:, n, :], banks[n % 2][:, :], ALU.add)\
                        .then_inc(m["o_add"], 1)

            for k in range(KC):
                dve.wait_ge(m["x_hi"], k + 1)
                split_lo(xT[:, 1, k], raw_x[:, k], xT[:, 0, k]).then_inc(m["x_lo"], 1)
                if k < 3:
                    w_low(0, k)
            wo_low(0)
            for j in range(3):
                w_low(1, j)
            v_evac(0)
            dve.wait_ge(in_const, 16 * 8)
            for p in range(NP_):
                for g in range(4):
                    n = 4 * p + g
                    dve.wait_ge(m["s_mm"], n + 1)
                    if p >= 1:
                        dve.wait_ge(m["pt_mm"], n - 3)
                        dve.wait_ge(m["exp_ok"], n - 3)
                    sc = banks[2 + g % 2][0:S, 0:HALF].rearrange("p (a c) -> p a c", a=BH)
                    nc.vector.scalar_tensor_tensor(prob[0:S, g], sc, -SCALE,
                                                   causal[0:S, :].unsqueeze(1).to_broadcast([S, BH, S]),
                                                   ALU.mult, ALU.subtract).then_inc(m["masked"], 1)
                    dve.wait_ge(m["masked"], n + 1)
                    nc.vector.tensor_reduce(neg_max[0:S, g * BH:(g + 1) * BH], prob[0:S, g], AX.X, ALU.min)\
                        .then_inc(m["neg_max_ok"], 1)
                if p >= 1:
                    add_out(p - 1)
                    wo_low(p)
                dve.wait_ge(m["exp_ok"], 4 * p + 4)
                if p >= 1:
                    dve.wait_ge(m["prob_ok"], 4 * p)
                nc.vector.reciprocal(exp_inv[0:S, :], exp_sum[0:S, :]).then_inc(m["inv_ok"], 1)
                dve.wait_ge(m["inv_ok"], p + 1)
                for g in range(4):
                    nc.vector.tensor_tensor(prob[0:S, g], prob[0:S, g],
                                            exp_inv[0:S, g * BH:(g + 1) * BH].unsqueeze(2).to_broadcast([S, BH, S]),
                                            ALU.mult).then_inc(m["prob_ok"], 1)
                if p + 2 < NP_:
                    for j in range(3):
                        w_low(p + 2, j)
                if p + 1 < NP_:
                    v_evac(p + 1)
                else:
                    for k in range(KC):
                        dve.wait_ge(m["kv_hi"], k + 1)
                        split_lo(w_kv[:, 1, k], raw_kv[k // 2][:, k % 2], w_kv[:, 0, k]).then_inc(m["kv_lo"], 1)

                def pt(g):
                    n = 4 * p + g
                    dve.wait_ge(m["pt_mm"], n + 1)
                    if n >= 2:
                        dve.wait_ge(m["z_mm"], n - 1)
                    nc.vector.tensor_copy(probT[0:S, g % 2], banks[4 + g % 2][0:S, 0:HALF]
                                          .rearrange("p (a c) -> p a c", a=BH)).then_inc(m["pt_out"], 1)

                def z(g):
                    n, h, hf = 4 * p + g, g // 2, g % 2
                    dve.wait_ge(m["z_hi"], n + 1)
                    split_lo(zT[:, 1, h, hf * HALF:(hf + 1) * HALF], banks[6 + g % 2][:, 0:HALF],
                             zT[:, 0, h, hf * HALF:(hf + 1) * HALF]).then_inc(m["z_lo"], 1)

                pt(0)
                pt(1)
                pt(2)
                z(0)
                pt(3)
                z(1)
                z(2)
                z(3)
            add_out(NP_ - 1)

            def c_low(b):
                dve.wait_ge(m["c_hi"], b + 1)
                split_lo(cT[b % 2][:, 1], raw_c[b % 2], cT[b % 2][:, 0]).then_inc(m["c_lo"], 1)

            def stats(n, ln, added):
                dve.wait_ge(*added)
                if ln:
                    dve.wait_ge(m["mv_ok"], NT * (ln - 1) + n + 1)
                nc.vector.bn_stats(ln_st[:, n, :], acc[:, n, :]).then_inc(m["bn_ok"], 1)

            def normalise(ln):
                for n in range(NT):
                    dve.wait_ge(m["bn_ok"], NT * ln + n + 1)
                    if ln:
                        dve.wait_ge(m["ln_ok"], NT * ln)
                    nc.vector.bn_aggr(ln_mv[:, n, :], ln_st[:, n, :]).then_inc(m["mv_ok"], 1)
                dve.wait_ge(m["mv_ok"], NT * (ln + 1))
                if ln:
                    dve.wait_ge(m["sd_ok"], ln)
                nc.vector.tensor_scalar(ln_ve[:, :], ln_mv[:, :, 1], LN_EPS, None, ALU.add).then_inc(m["ve_ok"], 1)
                dve.wait_ge(m["sd_ok"], ln + 1)
                nc.vector.reciprocal(ln_rs[:, :], ln_sd[:, :]).then_inc(m["rs_ok"], 1)
                dve.wait_ge(m["rs_ok"], ln + 1)
                for n in range(NT):
                    nc.vector.tensor_scalar(acc[:, n, :], acc[:, n, :], ln_mv[:, n, 0:1], ln_rs[:, n:n + 1],
                                            ALU.subtract, ALU.mult).then_inc(m["ln_ok"], 1)

            def turned_lo(n, i, bank):
                dve.wait_ge(m["t_hi"], i + 1)
                split_lo(xT[:, 1, :, n * P:(n + 1) * P], banks[bank][:, :].rearrange("p (k c) -> p k c", k=KC),
                         xT[:, 0, :, n * P:(n + 1) * P]).then_inc(m["t_lo"], 1)

            def x3_low(j, dst):
                dve.wait_ge(m["x3_hi"], j + 1)
                split_lo(dst[:, 1], raw_x3, dst[:, 0]).then_inc(m["x3_lo"], 1)

            c_low(0)
            c_low(1)
            for n in range(NCT):
                b, c = n // CT, n % CT
                dve.wait_ge(m["ck_exp"], n + 1)
                if n >= 3:
                    dve.wait_ge(m["sum_mm"], n - 2)
                nc.vector.scalar_tensor_tensor(phi_k[0:CM, n % 3, :], exp_c[0:CM, n % 2, :], 1.0,
                                               relu_c[0:CM, n % 2, :], ALU.min, ALU.add).then_inc(m["phi_ok"], 1)
                dve.wait_ge(m["cv_mm"], n + 1)
                nc.vector.tensor_copy(v_c[0:CM, n % 3, :], banks[2 + n % 2][0:CM, :]).then_inc(m["cv_out"], 1)
                if c == 0 and b >= 1:
                    dve.wait_ge(m["sum_mm"], CT * b)
                    nc.vector.tensor_tensor(kv_sum[:, b - 1], banks[4 + (b - 1) % 2][:, :]
                                            .rearrange("p (k c) -> p k c", k=KC),
                                            blocks[:, :].unsqueeze(1).to_broadcast([P, KC, P]), ALU.mult)\
                        .then_inc(m["sum_out"], 1)
                    nc.vector.tensor_copy(k_sum[:, b - 1, :], banks[6][:, 0:KC]).then_inc(m["sum_out"], 1)
                if c == CT - 1:
                    if b == 0:
                        for j in range(NT):
                            stats(j, 0, (m["o_add"], NT * (NP_ - 1) + j + 1))
                        normalise(0)
                        dve.wait_ge(m["rt_ok"], 1)
                        split_lo(rt_lo[:, :, :], rt_w[:, :, :], rt_hi[:, :, :]).then_inc(m["rt_ok"], 1)
                        nc.vector.tensor_scalar(gu_b[:, :, KC:2 * KC], gu_b[:, :, KC:2 * KC], 1.0, None, ALU.add)\
                            .then_inc(m["gub_ok"], 1)
                    if b >= 1:
                        turned_lo(b - 1, b - 1, 7)
                    if b in (1, 3):
                        x3_low(b // 2, (w_q, w_g)[b // 2])
                    if b + 2 < NB:
                        c_low(b + 2)
            b = NB
            dve.wait_ge(m["sum_mm"], CT * b)
            nc.vector.tensor_tensor(kv_sum[:, b - 1], banks[4 + (b - 1) % 2][:, :].rearrange("p (k c) -> p k c", k=KC),
                                    blocks[:, :].unsqueeze(1).to_broadcast([P, KC, P]), ALU.mult)\
                .then_inc(m["sum_out"], 1)
            nc.vector.tensor_copy(k_sum[:, b - 1, :], banks[6][:, 0:KC]).then_inc(m["sum_out"], 1)

            for j in range(2 * KC):
                g, hf = j // 2, j % 2
                dve.wait_ge(m["q2_act"], j + 1)
                nc.vector.scalar_tensor_tensor(phi_q[:, g, hf * HALF:(hf + 1) * HALF], exp_q[:, j % 2, :], 1.0,
                                               relu_q[:, j % 2, :], ALU.min, ALU.add).then_inc(m["q2_phi"], 1)
            x3_low(2, w_xo)
            for b in range(NB):
                at = atn[:, b % 2]
                den = banks[6 + b % 2][:, 0:HALF].rearrange("p (k c) -> p k c", k=KC)
                num = banks[4 + b % 2][:, 0:HALF].rearrange("p (k c) -> p k c", k=KC)
                dve.wait_ge(m["a_mm"], b + 1)
                if b >= 2:
                    dve.wait_ge(m["a_lo"], b - 1)
                if b == 0:
                    dve.wait_ge(m["q2_phi"], 2 * KC)
                nc.vector.tensor_scalar(at, den, DEN_EPS, None, ALU.add).then_inc(m["a_den"], 1)
                dve.wait_ge(m["a_den"], b + 1)
                nc.vector.reciprocal(at, at).then_inc(m["a_inv"], 1)
                dve.wait_ge(m["a_inv"], b + 1)
                nc.vector.tensor_tensor(at, num, at, ALU.mult).then_inc(m["a_num"], 1)
                dve.wait_ge(m["a_num"], b + 1)
                dve.wait_ge(m["g2_sig"], 2 * KC)
                nc.vector.tensor_tensor(at, at, sig[:, :, b * S:(b + 1) * S], ALU.mult).then_inc(m["a_gate"], 1)
                dve.wait_ge(m["a_hi"], b + 1)
                split_lo(aT[:, 1, :, b * S:(b + 1) * S], at, aT[:, 0, :, b * S:(b + 1) * S]).then_inc(m["a_lo"], 1)

            def gu_low(e, k):
                dve.wait_ge(m["gu_hi"], KC * e + k + 1)
                split_lo(w_gu[e % 2][:, 1, k], raw_gu[:, k], w_gu[e % 2][:, 0, k]).then_inc(m["gu_lo"], 1)

            for n in range(NT):
                dve.wait_ge(m["xo_mm"], n + 1)
                dve.wait_ge(m["ln_ok"], n + 1)
                nc.vector.tensor_tensor(acc[:, n, :], acc[:, n, :], banks[2 + n % 2][:, :], ALU.add)\
                    .then_inc(m["xo_add"], 1)
            for n in range(NT):
                stats(n, 1, (m["xo_add"], n + 1))
            normalise(1)
            for k in range(KC):
                gu_low(0, k)
            for n in range(NT):
                turned_lo(n, NT + n, 4 + n % 2)
            x3_low(3, w_dn)
            dve.wait_ge(m["r_mm"], NT)
            nc.vector.tensor_tensor(logit[:, :, :], banks[6][:, 0:NT * NE].rearrange("p (n e) -> p n e", n=NT),
                                    rt_b[:, :].unsqueeze(1).to_broadcast([P, NT, NE]), ALU.add)\
                .then_inc(m["log_ok"], 1)
            for n in range(NT):
                dve.wait_ge(m["log_ok"], 1)
                nc.vector.max(top[:, n, :], logit[:, n, :]).then_inc(m["top_ok"], 1)
            for n in range(NT):
                dve.wait_ge(m["top_ok"], n + 1)
                nc.vector.max_index(top_i[:, n, :], top[:, n, :], logit[:, n, :]).then_inc(m["idx_ok"], 1)
            dve.wait_ge(m["idx_ok"], NT)
            nc.vector.tensor_copy(top_f[:, :, :], top_i[:, :, 0:2]).then_inc(m["topf_ok"], 1)
            nc.vector.tensor_tensor(top_d[:, :, 0:1], top[:, :, 0:1], top[:, :, 1:2], ALU.subtract)
            nc.vector.tensor_tensor(top_d[:, :, 1:2], top[:, :, 1:2], top[:, :, 0:1], ALU.subtract)\
                .then_inc(m["topd_ok"], NT)
            dve.wait_ge(m["topw_ok"], 1)
            dve.wait_ge(m["topf_ok"], 1)
            for n in range(NT):
                if n:
                    dve.wait_ge(m["score_ok"], n)
                for j in range(2):
                    nc.vector.tensor_scalar(pick[:, j, :], iota[:, :], top_f[:, n, j:j + 1], top_w[:, n, j:j + 1],
                                            ALU.is_equal, ALU.mult).then_inc(m["pick_ok"], 1)
                dve.wait_ge(m["pick_ok"], 2 * n + 2)
                nc.vector.tensor_tensor(score[:, n, :], pick[:, 0, :], pick[:, 1, :], ALU.add)\
                    .then_inc(m["score_ok"], 1)
            for n in range(NT):
                dve.wait_ge(m["db_mm"], n + 1)
                nc.vector.tensor_tensor(acc[:, n, :], acc[:, n, :], banks[2 + n % 2][:, :], ALU.add)\
                    .then_inc(m["db_add"], 1)

            def h_low(n):
                i, c = n // KC, n % KC
                N = TOKN[i % 2]
                dve.wait_ge(m["h_hi"], n + 1)
                split_lo(hT[:, 1, c, 0:N], hh[:, n % 2, 0:N], hT[:, 0, c, 0:N]).then_inc(m["h_lo"], 1)

            def clamp(n):
                e, i, c = n // (2 * KC), n // KC, n % KC
                N = TOKN[i % 2]
                dve.wait_ge(m["gu_mm"], n + 1)
                if n >= 2:
                    dve.wait_ge(m["pr_ok"], n - 1)
                if n == 0:
                    dve.wait_ge(m["gub_ok"], 1)
                nc.vector.tensor_scalar(gl[:, n % 2, 0:N], banks[n % 2][:, 0:N], gu_b[:, e, c:c + 1], LIMIT,
                                        ALU.add, ALU.min).then_inc(m["gl_ok"], 1)
                if n >= 2:
                    dve.wait_ge(m["hh_ok"], n - 1)
                nc.vector.tensor_scalar(up[:, n % 2, 0:N], banks[2 + n % 2][:, 0:N],
                                        gu_b[:, e, KC + c:KC + c + 1], LIMIT + 1, ALU.add, ALU.min)\
                    .then_inc(m["up_ok"], 1)

            def hidden(n):
                i = n // KC
                N = TOKN[i % 2]
                dve.wait_ge(m["pr_ok"], n + 1)
                dve.wait_ge(m["up_ok"], n + 1)
                if n >= 2:
                    dve.wait_ge(m["h_lo"], n - 1)
                nc.vector.scalar_tensor_tensor(hh[:, n % 2, 0:N], up[:, n % 2, 0:N], 1 - LIMIT, pr[:, n % 2, 0:N],
                                               ALU.max, ALU.mult).then_inc(m["hh_ok"], 1)

            def add_down(i):
                e, hf = i // 2, i % 2
                for j in range(TOKN[hf] // P):
                    tt = 4 * hf + j
                    n = e * NT + tt
                    dve.wait_ge(m["dn_mm"], n + 1)
                    if e:
                        dve.wait_ge(m["dn_add"], n + 1 - NT)
                    else:
                        dve.wait_ge(m["db_add"], tt + 1)
                    nc.vector.scalar_tensor_tensor(acc[:, tt, :], banks[4 + n % 4][:, :], score[:, tt, e:e + 1],
                                                   acc[:, tt, :], ALU.mult, ALU.add).then_inc(m["dn_add"], 1)

            NN = 2 * NE * KC
            for n in range(NN):
                i, c, e = n // KC, n % KC, n // (2 * KC)
                clamp(n)
                if c == 1 and i >= 1:
                    add_down(i - 1)
                if n >= 1:
                    hidden(n - 1)
                    h_low(n - 1)
                if n % (2 * KC) == 4 and e >= 1:
                    x3_low(3 + e, w_dn)
                if e + 1 < NE and n % (2 * KC) in (2, 3, 4, 6):
                    gu_low(e + 1, (2, 3, 4, 6).index(n % (2 * KC)))
            hidden(NN - 1)
            h_low(NN - 1)
            add_down(2 * NE - 1)
            for n in range(NT):
                stats(n, 2, (m["dn_add"], NT * (NE - 1) + n + 1))
            normalise(2)


def kernel(x, ctx_2048, L0_attn_W_Q, L0_attn_W_K, L0_attn_W_V, L0_attn_W_O, L0_xattn_Wq, L0_xattn_Wg, L0_xattn_bg,
           L0_xattn_Wkv, L0_xattn_Wo, L0_ffn_router_weight, L0_ffn_router_bias, L0_ffn_gate_up_proj,
           L0_ffn_gate_up_proj_bias, L0_ffn_down_proj, L0_ffn_down_proj_bias):
    import numpy as np
    import concourse.bacc as _bacc
    from concourse.bass_utils import run_bass_kernel_spmd as _run

    def arr(a):
        return np.asarray(a)

    NB, S, D = x.shape
    T, KC = NB * S, D // P
    H = L0_attn_W_Q.shape[0]

    def cols(w, parts=KC):
        return arr(w).T.reshape(parts, P, -1).transpose(1, 0, 2)

    def pairs(w):
        return arr(w).reshape(H // 2, 2 * P, KC, P).transpose(0, 3, 2, 1)

    gu = arr(L0_ffn_gate_up_proj)
    NE = gu.shape[0]
    gub = arr(L0_ffn_gate_up_proj_bias).reshape(NE, D, 2)
    causal = np.where(np.arange(S)[None, :] > np.arange(P)[:, None], np.float32(NEG), np.float32(0))
    blocks = (np.arange(P)[:, None] // 32 == np.arange(P)[None, :] // 32).astype(np.float32)
    arrays = {
        "x": arr(x),
        "x_t": cols(arr(x).reshape(T, D)),
        "w_qkv": np.stack([pairs(L0_attn_W_Q), pairs(L0_attn_W_K), pairs(L0_attn_W_V)], 2),
        "w_o": arr(L0_attn_W_O).reshape(H // 2, 2, D, P).transpose(0, 3, 1, 2),
        "ctx_t": arr(ctx_2048).transpose(0, 2, 1).reshape(NB, KC, P, -1).transpose(0, 2, 1, 3),
        "w_kv": cols(L0_xattn_Wkv),
        "w_x3": np.stack([cols(L0_xattn_Wq), cols(L0_xattn_Wg), cols(L0_xattn_Wo)]),
        "gate_b": arr(L0_xattn_bg).reshape(KC, P).T,
        "rt_w": cols(L0_ffn_router_weight),
        "rt_b": np.broadcast_to(arr(L0_ffn_router_bias), (P, NE)),
        "w_gu": np.concatenate([gu[:, :, 0::2], gu[:, :, 1::2]], 2).reshape(NE, KC, P, -1).transpose(0, 2, 1, 3),
        "gu_b": np.concatenate([gub[:, :, 0].reshape(NE, KC, P), gub[:, :, 1].reshape(NE, KC, P)], 1).transpose(2, 0, 1),
        "w_down": arr(L0_ffn_down_proj).reshape(NE, KC, P, D).transpose(0, 2, 1, 3),
        "dn_b": arr(L0_ffn_down_proj_bias),
        "ident": np.eye(P, dtype=np.float32),
        "causal": causal,
        "blocks": blocks,
        "iota": np.broadcast_to(np.arange(NE, dtype=np.float32), (P, NE)),
    }
    nc = _bacc.Bacc("TRN2", target_bir_lowering=False, num_devices=1)
    feed, args = {}, {}
    for name, a in arrays.items():
        a = np.ascontiguousarray(a)
        feed[f"in_{name}_dram"] = a
        args[name] = nc.dram_tensor(f"in_{name}_dram", a.shape, mybir.dt.from_np(a.dtype), kind="ExternalInput").ap()
    out = nc.dram_tensor("out_0_dram", (NB, S, D), F32, kind="ExternalOutput").ap()
    decoder_layer(nc, args, out)
    res = _run(nc, [feed], core_ids=[0])
    return res.results[0]["out_0_dram"]
```

```python
from contextlib import ExitStack

import concourse.bass as bass
from concourse import mybir

ALU = mybir.AluOpType
ACT = mybir.ActivationFunctionType
AX = mybir.AxisListType
F32 = mybir.dt.float32
F32R = mybir.dt.float32r
U32 = mybir.dt.uint32

P = 128
LN_EPS, DEN_EPS = 1e-5, 1e-6
ALPHA, LIMIT = 1.702, 7.0
NEG = -1e9
CAP = 288
R_LEN, F_LEN = 30720, 20096


def decoder_layer(nc: bass.Bass, t: dict, out: bass.AP):
    NB, S, D = t["x"].shape
    T = NB * S
    KC = D // P
    NP_ = t["w_qkv"].shape[0]
    E = P
    HALF = T // 2
    NT = T // P
    SC = t["ctx_t"].shape[3]
    CT = 3
    CM = SC // CT
    NE = t["w_gu"].shape[0]
    FI = t["w_down"].shape[2] * 1
    BH = NB // 2
    SCALE = float(E) ** -0.5
    NCT = NB * CT
    TOK0 = [0, 4 * P]
    TOKN = [4 * P, T - 4 * P]

    with ExitStack() as ctx:
        def sb(name, shape, dt=F32):
            return ctx.enter_context(nc.sbuf_tensor(name, shape, dt))

        def sem(name):
            return ctx.enter_context(nc.semaphore(name))

        R_AT = (nc.sbuf_base + 63) // 64 * 64
        sb("arena", [P, R_LEN + F_LEN + 16])
        R = nc.alloc_sbuf_tensor_at("R", [P, R_LEN], F32R, offset=R_AT)
        F = nc.alloc_sbuf_tensor_at("F", [P, F_LEN], F32, offset=R_AT + 4 * R_LEN)
        R2 = nc.alloc_sbuf_tensor_at("R2", [P, 4320], F32R, offset=R_AT + 4 * (R_LEN + 13056))
        ident = sb("ident", [P, P])
        causal = sb("causal", [P, S])
        blocks = sb("blocks", [P, P])
        iota = sb("iota", [P, NE])
        ones = sb("ones", [P, 2])
        y_row = sb("y_row", [P, NT, 2], U32)
        pick_slot = sb("pick_slot", [P, NT, 2])
        near = sb("near", [P, NT, 2])
        here = sb("here", [P, NT, 2])
        w_now = sb("w_now", [P, NT, 2])
        hot = sb("hot", [P, 2, NT, NE])
        chosen = sb("chosen", [P, NT, NE])
        rank = sb("rank", [P, NT, NE])
        slot_of = sb("slot_of", [P, 4, NE, NT])
        most = sb("most", [P, 5])
        more_i = sb("more_i", [P, 1], U32)
        tick = sb("tick", [P, 1])
        slot_now = sb("slot_now", [P, NT])
        more_slot = sb("more_slot", [P, NT])
        more_b = sb("more_b", [P, 2 * KC])
        y_dram = nc.dram_tensor("y_rows", (NE * CAP, D), F32, kind="Internal").ap()
        slot_dram = nc.dram_tensor("slot_rows", (3 * NE, P, NT), F32, kind="Internal").ap()
        neg_max = sb("neg_max", [P, 16])
        exp_sum = sb("exp_sum", [P, 16])
        exp_inv = sb("exp_inv", [P, 16])
        ln_st = sb("ln_st", [P, NT, 6])
        ln_mv = sb("ln_mv", [P, NT, 2])
        ln_ve = sb("ln_ve", [P, NT])
        ln_sd = sb("ln_sd", [P, NT])
        ln_rs = sb("ln_rs", [P, NT])
        k_sum = sb("k_sum", [P, NB, KC])
        gate_b = sb("gate_b", [P, KC])
        rt_w = sb("rt_w", [P, KC, NE])
        rt_b = sb("rt_b", [P, NE])
        logit = sb("logit", [P, NT, NE])
        top = sb("top", [P, NT, 8])
        top_i = sb("top_i", [P, NT, 8], U32)
        top_f = sb("top_f", [P, NT, 2])
        top_d = sb("top_d", [P, NT, 2])
        top_w = sb("top_w", [P, NT, 2])
        pick = sb("pick", [P, 2, NT, NE])
        score = sb("score", [P, NT, NE])
        gu_b = sb("gu_b", [P, NE, 2 * KC])
        banks = [ctx.enter_context(nc.psum_tensor(f"bank{i}", [P, 512], F32)) for i in range(8)]

        def r(at, shape):
            n = 1
            for s in shape:
                n *= s
            v = R[:, at:at + 2 * n]
            if len(shape) == 1:
                return v.rearrange("p (o a) -> p o a", o=2)
            return v.rearrange("p (o a b) -> p o a b", o=2, a=shape[0])

        def f(at, *shape):
            n = 1
            for s in shape:
                n *= s
            v = F[:, at:at + n]
            if len(shape) == 1:
                return v
            if len(shape) == 2:
                return v.rearrange("p (a b) -> p a b", a=shape[0])
            return v.rearrange("p (a b c) -> p a b c", a=shape[0], b=shape[1])

        def bits(ap):
            return ap.bitcast(F32)

        xT = r(0, (KC, T))
        w_qkv = [[r(7168 + 6144 * s + 2048 * j, (KC, 2 * E)) for j in range(3)] for s in range(2)]
        zT = r(19456, (2, T))
        w_o = r(23040, (2, D))
        w_kv = r(7168, (KC, 2 * D))
        cT = [r(15360, (KC, SC)), r(19456, (KC, SC))]
        w_q = r(22456, (KC, D))
        w_g = r(26552, (KC, D))
        w_xo = r(7168, (KC, D))
        aT = r(23552, (KC, T))
        w_gu = [r(15360, (KC, 2 * D)), r(7168, (KC, 2 * D))]
        w_dn = r(23552, (KC, D))
        hT = r(27648, (KC, CAP))
        x_n = r(0, (NT, D))
        x_g = R2[:, 2016:4320].rearrange("p (o a b) -> p o a b", o=2, a=KC)
        sel = R2[:, 0:2016].rearrange("p (n c) -> p n c", n=NT)
        raw_w = f(0, 3, KC, 2 * E)
        raw_o = f(3072, 2, D)
        acc = f(4096, NT, D)
        qT = f(7680, 2, T)
        kT = f(9472, 2, T)
        prob = f(11264, 4, BH, S)
        probT = f(13056, 2, BH, S)
        V = f(13952, 2, NB, 2 * E)
        raw_x = f(13952, KC, T)
        raw_kv = [f(0, 2, 2 * D), f(18048, 2, 2 * D)]
        raw_c = [f(0, KC, SC), f(1500, KC, SC)]
        phi_k = f(7680, 3, D)
        v_c = f(9216, 3, KC, P + 2)
        relu_c = f(10776, 2, D)
        exp_c = f(11800, 2, D)
        kv_sum = f(13952, NB, KC, P)
        raw_x3 = f(18048, KC, D)
        phi_q = f(7680, KC, T)
        relu_q = f(11264, 2, HALF)
        exp_q = f(12160, 2, HALF)
        sig = f(0, KC, T)
        k_blk = f(11264, 2, KC, P)
        atn = f(12288, 2, KC, S)
        raw_gu = f(0, KC, 2 * D)
        gl = f(7680, 2, CAP)
        sg = f(8256, 2, CAP)
        up = f(8832, 2, CAP)
        pr = f(9408, 2, CAP)
        hh = f(9984, 2, CAP)
        y = f(10560, 3, D)
        dn_b = f(12096, D)
        iota_c = f(12608, CAP)
        x2T = f(7680, 2, KC, P)
        scoreT = f(8704, T)
        before = f(9600, P)
        all_ones = f(9728, P)
        y_got = f(0, 8, D)

        in_const = sem("in_const")
        in_x = [sem(f"in_xt{k}") for k in range(KC)]
        in_acc = sem("in_acc")
        in_w = [sem(f"in_w{j}") for j in range(3)]
        in_wo = sem("in_wo")
        in_kv = [sem(f"in_kv{j}") for j in range(2)]
        in_c = [sem(f"in_c{j}") for j in range(2)]
        in_x3 = sem("in_x3")
        in_gu = sem("in_gu")
        in_dnb = sem("in_dnb")
        in_m = sem("in_m")
        in_more = sem("in_more")
        slot_out = sem("slot_out")
        y_done = sem("y_done")
        y_in = [sem(f"y_in{i}") for i in range(8)]
        out_done = sem("out_done")
        names = """ones_set ones_col x_hi x_lo w_hi w_lo wo_hi wo_lo q_mm v_mm qk_out v_out s_mm masked neg_max_ok exp_ok inv_ok
            prob_ok pt_mm pt_out z_mm z_hi z_lo o_mm o_add kv_hi kv_lo c_hi c_lo ck_mm cv_mm ck_relu ck_exp
            phi_ok cv_out sum_mm sum_out bn_ok mv_ok ve_ok sd_ok rs_ok ln_ok t_mm t_hi t_lo
            x3_hi x3_lo q2_mm q2_act q2_phi g2_mm g2_sig blk_ok a_mm a_den a_inv a_num a_gate a_hi a_lo xo_mm xo_add
            rt_ok r_mm log_ok top_ok idx_ok topf_ok topd_ok topw_ok pick_ok score_ok st_mm st_out db_mm db_add
            gub_ok gu_hi gu_lo gu_mm gl_ok up_ok sg_ok pr_ok hh_ok h_hi h_lo dn_mm
            now_ok now_slot near_ok here_ok w_ok n_hi n_lo x2t_out hot_ok chosen_ok rank_mm rank_ok slot_ok level_ok row_ok more_ok moreb_ok sel_ok
            xg_mm xg_hi xg_lo y_out comb""".split()
        m = {n: sem(n) for n in names}

        block = ctx.enter_context(nc.Block())

        PASSES = ((0, 0), (0, 1), (1, 0))

        def products(mm_out, lhs, rhs, n):
            for k in range(n):
                for i, (a, b) in enumerate(PASSES):
                    last = nc.tensor.matmul(mm_out, lhs(a, k), rhs(b, k), start=(k == 0 and i == 0),
                                            stop=(k == n - 1 and i == 2))
            return last

        @block.sync
        def _(sp):
            def y_store(c, e):
                sp.wait_ge(m["y_out"], 3 * c + 3)
                for k, (p0, rows) in enumerate(((0, P), (0, P), (3 * P - CAP, CAP - 2 * P))):
                    sp.dma_start(y_dram[bass.ds(e * CAP + k * P, rows), :], y[p0:p0 + rows, k, :])\
                        .then_inc(y_done, 16)

            for k in range(KC):
                sp.dma_start(raw_x[:, k, :], t["x_t"][:, k, :]).then_inc(in_x[k], 16)
                if k < 3:
                    sp.dma_start(raw_w[:, k], t["w_qkv"][0, :, k]).then_inc(in_w[k], 16)
            for dst, src in ((ident, "ident"), (causal, "causal"), (blocks, "blocks"), (iota, "iota"),
                             (gate_b, "gate_b"), (rt_b, "rt_b")):
                sp.dma_start(dst[:, :], t[src]).then_inc(in_const, 16)
            sp.dma_start(rt_w[:, :, :], t["rt_w"]).then_inc(in_const, 16)
            sp.dma_start(gu_b[:, :, :], t["gu_b"]).then_inc(in_const, 16)
            sp.dma_start(raw_o, t["w_o"][0]).then_inc(in_wo, 16)
            sp.dma_start(acc, t["x"].rearrange("b s d -> (b s) d").rearrange("(n p) d -> p n d", p=P)).then_inc(in_acc, 16)
            for p in range(1, NP_):
                for j in range(3):
                    sp.wait_ge(m["w_lo"], 3 * (p - 1) + j + 1)
                    sp.dma_start(raw_w[:, j], t["w_qkv"][p, :, j]).then_inc(in_w[j], 16)
                if p >= 1:
                    sp.wait_ge(m["wo_lo"], p)
                    sp.dma_start(raw_o, t["w_o"][p]).then_inc(in_wo, 16)
            sp.wait_ge(m["w_lo"], 3 * NP_)
            sp.dma_start(raw_kv[0], t["w_kv"][:, 0:2]).then_inc(in_kv[0], 16)
            sp.dma_start(raw_kv[1], t["w_kv"][:, 2:4]).then_inc(in_kv[1], 16)
            sp.wait_ge(m["kv_lo"], KC)
            sp.dma_start(raw_x3, t["w_x3"][0]).then_inc(in_x3, 16)
            for b in range(NB):
                if b >= 2:
                    sp.wait_ge(m["c_lo"], b - 1)
                sp.dma_start(raw_c[b % 2], t["ctx_t"][b]).then_inc(in_c[b % 2], 16)
                if b in (3, 5):
                    j = (b - 1) // 2
                    sp.wait_ge(m["x3_lo"], j)
                    sp.dma_start(raw_x3, t["w_x3"][j]).then_inc(in_x3, 16)
            sp.wait_ge(m["a_lo"], NB)
            for dst, src in ((dn_b[0:NE, :], "dn_b"), (iota_c, "iota_c"), (before, "before"), (all_ones, "all_ones")):
                sp.dma_start(dst, t[src]).then_inc(in_m, 16)
            for e in range(NE):
                if e:
                    sp.wait_ge(m["gu_lo"], KC * e)
                sp.dma_start(raw_gu, t["w_gu"][e]).then_inc(in_gu, 16)
                sp.wait_ge(m["x3_lo"], 3 + e)
                sp.dma_start(raw_x3, t["w_down"][e]).then_inc(in_x3, 16)
                if e:
                    y_store(e - 1, e - 1)
            y_store(NE - 1, NE - 1)

            def more(c, j, e):
                sp.wait_ge(m["comb"], j * (2 * NT) + 2 * NT)
                sp.wait_ge(m["y_out"], 3 * c)
                sp.dma_start(raw_gu, t["w_gu"][e]).then_inc(in_gu, 16)
                sp.dma_start(raw_x3, t["w_down"][e]).then_inc(in_x3, 16)
                sp.dma_start(more_b[:, :], t["gu_b"].rearrange("p e c -> e p c")[e]).then_inc(in_more, 16)
                sp.dma_start(more_slot[:, :], slot_dram[j * NE + e]).then_inc(in_more, 16)
                y_store(c, e)

            sp.wait_ge(m["more_ok"], 1)
            rounds = sp.value_load(more_i[0:1, 0:1], min_val=0, max_val=3)
            with sp.If(rounds > 0):
                sp.dma_start(slot_dram.rearrange("r p n -> p r n"),
                             slot_of[:, 1:4].rearrange("p j e n -> p (j e) n")).then_inc(slot_out, 16)
                sp.wait_ge(slot_out, 16)
                with sp.Fori(0, rounds) as j:
                    with sp.Fori(0, NE) as e:
                        more(NE + j * NE + e, j, e)
            o = out.rearrange("b s d -> (b s) d").rearrange("(n p) d -> p n d", p=P)
            for n in range(NT):
                sp.wait_ge(m["ln_ok"], 2 * NT + n + 1)
                sp.dma_start(o[:, n, :], acc[:, n, :]).then_inc(out_done, 16)
            sp.wait_ge(out_done, 16 * NT)

        @block.gpsimd
        def _(pool):
            nc.gpsimd.memset(ones[:, :], 1.0).then_inc(m["ones_set"], 1)
            pool.wait_ge(m["q2_phi"], 2 * KC)
            for b in range(NB):
                if b >= 2:
                    pool.wait_ge(m["a_mm"], b - 1)
                pool.wait_ge(m["sum_out"], 4 * (b + 1))
                nc.gpsimd.tensor_tensor(k_blk[:, b % 2], blocks[:, :].unsqueeze(1).to_broadcast([P, KC, P]),
                                        k_sum[:, b, :].unsqueeze(2).to_broadcast([P, KC, P]),
                                        ALU.mult).then_inc(m["blk_ok"], 1)

            def select(c, slots):
                for n in range(NT):
                    nc.gpsimd.tensor_scalar(sel[:, n, :], iota_c, slots(n), None, ALU.is_equal)\
                        .then_inc(m["sel_ok"], 1)

            def gated(c):
                for q in range(KC):
                    n = KC * c + q
                    pool.wait_ge(m["sg_ok"], n + 1)
                    if not (isinstance(c, int) and n < 2):
                        pool.wait_ge(m["hh_ok"], n - 1)
                    nc.gpsimd.tensor_tensor(pr[:, q % 2], gl[:, q % 2], sg[:, q % 2], ALU.mult)\
                        .then_inc(m["pr_ok"], 1)

            pool.wait_ge(m["slot_ok"], 5)
            pool.wait_ge(in_m, 16 * 4)
            select(0, lambda n: slot_of[:, 0, 0, n:n + 1])
            for e in range(NE):
                if e + 1 < NE:
                    pool.wait_ge(m["xg_mm"], KC * (e + 1))
                    select(e + 1, lambda n: slot_of[:, 0, e + 1, n:n + 1])
                gated(e)

            def step():
                nc.gpsimd.tensor_tensor(tick[:, :], ones[:, 0:1], ones[:, 1:2], ALU.mult).then_inc(m["now_ok"], 1)
                pool.drain()

            def fetch(r, stored):
                later = not isinstance(r, int)
                pool.wait_ge(y_done, stored)
                if later:
                    step()
                pool.wait_ge(m["row_ok"], r + 1)
                if later:
                    step()
                for i in range(2 * NT):
                    if i >= 8:
                        pool.wait_ge(m["comb"], r * (2 * NT) + (i - 7))
                        if later:
                            step()
                    nc.gpsimd.indirect_dma_start(y_got[:, i % 8, :], None, y_dram,
                                                 bass.IndirectOffsetOnAxis(ap=y_row[:, i // 2, i % 2:i % 2 + 1], axis=0),
                                                 bounds_check=NE * CAP - 1, oob_is_err=True).then_inc(y_in[i % 8], 16)

            pool.wait_ge(m["gu_lo"], KC * NE)
            fetch(0, 48 * NE)
            pool.wait_ge(m["more_ok"], 1)
            rounds = pool.value_load(more_i[0:1, 0:1], min_val=0, max_val=3)
            with pool.If(rounds > 0):
                with pool.Fori(0, rounds) as j:
                    with pool.Fori(0, NE) as e:
                        c = NE + j * NE + e
                        pool.wait_ge(m["xg_mm"], KC * c)
                        pool.wait_ge(in_more, (j * NE + e) * 32 + 32)
                        nc.gpsimd.tensor_tensor(slot_now[:, :], more_slot[:, :], ones[:, 0:1].to_broadcast([P, NT]),
                                                ALU.mult).then_inc(m["now_ok"], 1)
                        pool.drain()
                        select(c, lambda n: slot_now[:, n:n + 1])
                        gated(c)
                    fetch(j + 1, j * (48 * NE) + 2 * 48 * NE)

        @block.tensor
        def _(pe):
            def scores(p):
                pe.wait_ge(m["qk_out"], 8 * (p + 1))
                for g in range(4):
                    h, hf, n = g // 2, g % 2, 4 * p + g
                    if n >= 2:
                        pe.wait_ge(m["masked"], n - 1)
                    for j in range(BH):
                        c = (hf * BH + j) * S
                        mm = nc.tensor.matmul(banks[2 + g % 2][0:S, j * S:(j + 1) * S], qT[:, h, c:c + S],
                                              kT[:, h, c:c + S], start=True, stop=True)
                    mm.then_inc(m["s_mm"], 1)

            def out_proj(p):
                pe.wait_ge(m["z_lo"], 4 * (p + 1))
                pe.wait_ge(m["wo_lo"], p + 1)
                for n in range(NT):
                    if n == 0:
                        pe.wait_ge(m["v_out"], 4 * min(p + 2, NP_))
                    if n >= 2:
                        pe.wait_ge(m["o_add"], NT * p + n - 1)
                    products(banks[n % 2][:, :], lambda a, k: zT[:, a, k, n * P:(n + 1) * P],
                             lambda b, k: w_o[:, b, k, :], 2).then_inc(m["o_mm"], 1)

            def proj(p):
                w = w_qkv[p % 2]
                for j in range(8):
                    part, h, hf = j // 4, (j // 2) % 2, j % 2
                    if p == 0 and j == 0:
                        pe.wait_ge(m["x_lo"], KC)
                    if j % 4 == 0:
                        pe.wait_ge(m["w_lo"], 3 * p + part + 1)
                    if j < 2 and p >= 2:
                        pe.wait_ge(m["o_add"], NT * (p - 2) + NT - 1 + j)
                    if j < 2 and p == 1:
                        pe.wait_ge(m["v_out"], 4)
                    if j >= 2:
                        pe.wait_ge(m["qk_out"], 8 * p + j - 1)
                    products(banks[(1 + j) % 2][:, 0:HALF], lambda a, k: w[part][:, a, k, h * E:(h + 1) * E],
                             lambda b, k: xT[:, b, k, hf * HALF:(hf + 1) * HALF], KC).then_inc(m["q_mm"], 1)

            def proj_v(p, j):
                if j == 0:
                    pe.wait_ge(m["w_lo"], 3 * p + 3)
                if j < 2:
                    pe.wait_ge(m["qk_out"], 8 * p + 7 + j)
                else:
                    pe.wait_ge(m["v_out"], 4 * p + j - 1)
                for i in range(2):
                    b0 = (2 * j + i) * S
                    mm = products(banks[(1 + j) % 2][0:S, i * 256:(i + 1) * 256],
                                  lambda a, k: xT[:, a, k, b0:b0 + S], lambda b, k: w_qkv[p % 2][2][:, b, k, :], KC)
                mm.then_inc(m["v_mm"], 1)

            def attend(p):
                def turn(g):
                    n = 4 * p + g
                    pe.wait_ge(m["prob_ok"], n + 1)
                    if n >= 2:
                        pe.wait_ge(m["pt_out"], n - 1)
                    for j in range(BH):
                        mm = nc.tensor.transpose(banks[4 + g % 2][0:S, j * S:(j + 1) * S], prob[0:S, g, j, :],
                                                 ident[0:S, 0:S])
                    mm.then_inc(m["pt_mm"], 1)

                def values(g):
                    n, h, hf = 4 * p + g, g // 2, g % 2
                    pe.wait_ge(m["pt_out"], n + 1)
                    if n >= 2:
                        pe.wait_ge(m["z_lo"], n - 1)
                    for j in range(BH):
                        mm = nc.tensor.matmul(banks[6 + g % 2][:, j * S:(j + 1) * S],
                                              V[0:S, p % 2, hf * BH + j, h * E:(h + 1) * E],
                                              probT[0:S, g % 2, j, :], start=True, stop=True)
                    mm.then_inc(m["z_mm"], 1)

                pe.wait_ge(m["v_out"], 4 * (p + 1))
                turn(0)
                turn(1)
                for g in range(4):
                    if p + 1 < NP_:
                        proj_v(p + 1, g)
                    values(g)
                    if g < 2:
                        turn(g + 2)

            def turn_acc(n, bank, ln, t_first, prev):
                pe.wait_ge(m["ln_ok"], NT * ln + n + 1)
                if prev:
                    pe.wait_ge(m["t_lo"], prev)
                for k in range(KC):
                    mm = nc.tensor.transpose(banks[bank][:, k * P:(k + 1) * P], acc[:, n, k * P:(k + 1) * P],
                                             ident[:, :])
                mm.then_inc(m["t_mm"], 1)

            proj(0)
            for j in range(4):
                proj_v(0, j)
            pe.wait_ge(in_const, 16 * 8)
            for p in range(NP_):
                scores(p)
                if p >= 1:
                    out_proj(p - 1)
                if p + 1 < NP_:
                    proj(p + 1)
                attend(p)
            out_proj(NP_ - 1)

            def sums(n):
                b, c = n // CT, n % CT
                pe.wait_ge(m["phi_ok"], n + 1)
                pe.wait_ge(m["cv_out"], n + 1)
                if c == 0 and b >= 1:
                    pe.wait_ge(m["sum_out"], 4 * b)
                if n == 0:
                    pe.wait_ge(m["ones_col"], 1)
                for g in range(KC):
                    mm = nc.tensor.matmul(banks[4 + g // 2][:, (g % 2) * (P + 1):(g % 2 + 1) * (P + 1)],
                                          phi_k[0:CM, n % 3, g * P:(g + 1) * P], v_c[0:CM, n % 3, g, 0:P + 1],
                                          start=(c == 0 and g % 2 == 0), stop=(c == CT - 1), skip_group_check=True)
                mm.then_inc(m["sum_mm"], 1)

            for n in range(NCT):
                b, c = n // CT, n % CT
                if c == 0:
                    pe.wait_ge(m["c_lo"], b + 1)
                if n == 0:
                    pe.wait_ge(m["kv_lo"], KC)
                    pe.wait_ge(m["o_add"], NT * NP_)
                if n >= 2:
                    pe.wait_ge(m["ck_exp"], n - 1)
                products(banks[n % 2][0:CM, :], lambda a, k: cT[b % 2][:, a, k, c * CM:(c + 1) * CM],
                         lambda q, k: w_kv[:, q, k, 0:D], KC).then_inc(m["ck_mm"], 1)
                if n >= 2:
                    pe.wait_ge(m["cv_out"], n - 1)
                products(banks[2 + n % 2][0:CM, :], lambda a, k: cT[b % 2][:, a, k, c * CM:(c + 1) * CM],
                         lambda q, k: w_kv[:, q, k, D:2 * D], KC).then_inc(m["cv_mm"], 1)
                if n >= 1:
                    sums(n - 1)
                if c == CT - 1 and b >= 1:
                    turn_acc(b - 1, 7, 0, 0, b - 1)
            sums(NCT - 1)

            pe.wait_ge(m["t_lo"], NT)
            pe.wait_ge(m["x3_lo"], 2)
            for n in range(4 * KC):
                j = n % (2 * KC)
                g, hf = j // 2, j % 2
                w = w_q if n < 2 * KC else w_g
                if n < 2:
                    pe.wait_ge(m["ck_exp"], NCT)
                elif n < 2 * KC + 2:
                    pe.wait_ge(m["q2_act"], n - 1)
                else:
                    pe.wait_ge(m["g2_sig"], n - 2 * KC - 1)
                products(banks[n % 2][:, 0:HALF], lambda a, k: w[:, a, k, g * P:(g + 1) * P],
                         lambda q, k: xT[:, q, k, hf * HALF:(hf + 1) * HALF], KC)\
                    .then_inc(m["q2_mm"] if n < 2 * KC else m["g2_mm"], 1)
            pe.wait_ge(m["q2_phi"], 2 * KC)
            pe.wait_ge(m["sum_out"], 4 * NB)
            for b in range(NB):
                pe.wait_ge(m["blk_ok"], b + 1)
                if b >= 2:
                    pe.wait_ge(m["a_num"], b - 1)
                for g in range(KC):
                    nc.tensor.matmul(banks[6 + b % 2][:, g * S:(g + 1) * S], k_blk[:, b % 2, g, :],
                                     phi_q[:, g, b * S:(b + 1) * S], start=True, stop=True)
                    mm = nc.tensor.matmul(banks[4 + b % 2][:, g * S:(g + 1) * S], kv_sum[:, b, g, :],
                                          phi_q[:, g, b * S:(b + 1) * S], start=True, stop=True)
                mm.then_inc(m["a_mm"], 1)
            pe.wait_ge(m["x3_lo"], 3)
            pe.wait_ge(m["cv_out"], NCT)
            for n in range(NT):
                pe.wait_ge(m["a_lo"], -(-(n + 1) * P // S))
                if n >= 2:
                    pe.wait_ge(m["xo_add"], n - 1)
                products(banks[2 + n % 2][:, :], lambda a, k: aT[:, a, k, n * P:(n + 1) * P],
                         lambda q, k: w_xo[:, q, k, :], KC).then_inc(m["xo_mm"], 1)
            def route(n):
                pe.wait_ge(m["x2t_out"], n + 1)
                for k in range(KC):
                    mm = nc.tensor.matmul(banks[6][:, n * NE:(n + 1) * NE], x2T[:, n % 2, k, :], rt_w[:, k, :],
                                          start=(k == 0), stop=(k == KC - 1))
                mm.then_inc(m["r_mm"], 1)

            for n in range(NT):
                pe.wait_ge(m["ln_ok"], NT + n + 1)
                if n >= 2:
                    pe.wait_ge(m["x2t_out"], n - 1)
                for k in range(KC):
                    mm = nc.tensor.transpose(banks[4 + n % 2][:, k * P:(k + 1) * P], acc[:, n, k * P:(k + 1) * P],
                                             ident[:, :])
                mm.then_inc(m["t_mm"], 1)
                if n >= 1:
                    route(n - 1)
            route(NT - 1)
            pe.wait_ge(m["chosen_ok"], 1)
            pe.wait_ge(in_m, 16 * 4)
            for n in range(NT):
                for i in range(n + 1):
                    nc.tensor.matmul(banks[7][:, n * NE:(n + 1) * NE], before if i == n else all_ones, chosen[:, i, :],
                                     start=(i == 0), stop=(i == n))
            for i in range(NT):
                mm = nc.tensor.matmul(banks[7][:, NT * NE:(NT + 1) * NE], all_ones, chosen[:, i, :],
                                      start=(i == 0), stop=(i == NT - 1))
            mm.then_inc(m["rank_mm"], 1)
            pe.wait_ge(m["score_ok"], 1)
            for n in range(NT):
                mm = nc.tensor.transpose(banks[n // 4][0:NE, (n % 4) * P:(n % 4 + 1) * P], score[:, n, :], ident[:, :])
            mm.then_inc(m["st_mm"], 1)
            pe.wait_ge(m["st_out"], 2)
            for n in range(NT):
                if n >= 2:
                    pe.wait_ge(m["db_add"], n - 1)
                nc.tensor.matmul(banks[2 + n % 2][:, :], scoreT[0:NE, n * P:(n + 1) * P], dn_b[0:NE, :],
                                 start=True, stop=True).then_inc(m["db_mm"], 1)

            def gather(c, downs):
                pe.wait_ge(m["sel_ok"], NT * c + NT)
                if downs is not None:
                    pe.wait_ge(m["y_out"], downs)
                for k in range(KC):
                    if not (isinstance(c, int) and KC * c + k < 2):
                        pe.wait_ge(m["xg_hi"], KC * c + (k - 1))
                        pe.wait_ge(m["xg_lo"], KC * c + (k - 1))
                    for a in range(2):
                        for n in range(NT):
                            mm = nc.tensor.matmul(banks[4 + 2 * (k % 2) + a][:, 0:CAP],
                                                  x_n[:, a, n, k * P:(k + 1) * P], sel[:, n, :],
                                                  start=(n == 0), stop=(n == NT - 1))
                    mm.then_inc(m["xg_mm"], 1)

            def gate_up(c, w):
                pe.wait_ge(m["gu_lo"], KC * c + KC)
                pe.wait_ge(m["xg_hi"], KC * c + KC)
                pe.wait_ge(m["xg_lo"], KC * c + KC)
                for q in range(KC):
                    if not (isinstance(c, int) and KC * c + q < 2):
                        pe.wait_ge(m["up_ok"], KC * c + (q - 1))
                    for h in range(2):
                        mm = products(banks[2 * h + q % 2][:, 0:CAP],
                                      lambda a, k: w[:, a, k, h * D + q * P:h * D + (q + 1) * P],
                                      lambda b, k: x_g[:, b, k, :], KC)
                    mm.then_inc(m["gu_mm"], 1)

            def down(c, gathered):
                pe.wait_ge(m["x3_lo"], c + 4)
                pe.wait_ge(m["h_lo"], KC * c + KC)
                pe.wait_ge(m["xg_hi"], gathered)
                pe.wait_ge(m["xg_lo"], gathered)
                for k, s0 in enumerate((0, P, CAP - P)):
                    products(banks[4 + k][:, :], lambda a, i: hT[:, a, i, s0:s0 + P],
                             lambda b, i: w_dn[:, b, i, :], KC).then_inc(m["dn_mm"], 1)

            pe.wait_ge(m["n_lo"], NT)
            pe.wait_ge(m["x2t_out"], NT)
            pe.wait_ge(m["log_ok"], 1)
            pe.wait_ge(m["rank_ok"], 2)
            gather(0, None)
            pe.wait_ge(m["db_add"], NT)
            for e in range(NE):
                gate_up(e, w_gu[e % 2])
                if e + 1 < NE:
                    gather(e + 1, 3 * e if e else None)
                down(e, KC * min(e + 2, NE))
            pe.wait_ge(m["more_ok"], 1)
            rounds = pe.value_load(more_i[0:1, 0:1], min_val=0, max_val=3)
            with pe.If(rounds > 0):
                with pe.Fori(0, rounds) as j:
                    with pe.Fori(0, NE) as e:
                        c = NE + j * NE + e
                        gather(c, 3 * c)
                        gate_up(c, w_gu[0])
                        down(c, KC * c + KC)

        @block.scalar
        def _(act):
            def split_hi(dst, src):
                return nc.scalar.copy(dst, src)

            def w_high(p, j):
                act.wait_ge(in_w[j], 16 * (p + 1))
                if p >= 2:
                    act.wait_ge(m["v_mm"], 4 * (p - 1))
                split_hi(w_qkv[p % 2][j][:, 0], raw_w[:, j]).then_inc(m["w_hi"], 1)

            def wo_high(p):
                act.wait_ge(in_wo, 16 * (p + 1))
                if p >= 1:
                    act.wait_ge(m["o_mm"], NT * p)
                split_hi(w_o[:, 0], raw_o).then_inc(m["wo_hi"], 1)

            def qk_evac(p, j):
                part, h, hf = j // 4, (j // 2) % 2, j % 2
                act.wait_ge(m["q_mm"], 8 * p + j + 1)
                if p >= 1:
                    act.wait_ge(m["s_mm"], 4 * p)
                dst = (qT, kT)[part]
                nc.scalar.copy(dst[:, h, hf * HALF:(hf + 1) * HALF], banks[(1 + j) % 2][:, 0:HALF])\
                    .then_inc(m["qk_out"], 1)

            for k in range(KC):
                act.wait_ge(in_x[k], 16)
                split_hi(xT[:, 0, k], raw_x[:, k]).then_inc(m["x_hi"], 1)
                if k < 3:
                    w_high(0, k)
            wo_high(0)
            for j in range(8):
                qk_evac(0, j)
                if j in (1, 3, 5):
                    w_high(1, j // 2)
            for p in range(NP_):
                for g in range(4):
                    act.wait_ge(m["neg_max_ok"], 4 * p + g + 1)
                    if g == 0 and p >= 1:
                        act.wait_ge(m["inv_ok"], p)
                    for j in range(BH):
                        i = g * BH + j
                        e = nc.scalar.activation(prob[0:S, g, j, :], prob[0:S, g, j, :], ACT.Exp,
                                                 bias=neg_max[0:S, i:i + 1], scale=-1.0,
                                                 accum_out=exp_sum[0:S, i:i + 1])
                    e.then_inc(m["exp_ok"], 1)
                if p >= 1:
                    wo_high(p)
                if p + 1 < NP_:
                    for j in range(8):
                        qk_evac(p + 1, j)
                        if j in (1, 3, 5) and p + 2 < NP_:
                            w_high(p + 2, j // 2)
                else:
                    act.wait_ge(m["v_mm"], 4 * NP_)
                    for k in range(KC):
                        act.wait_ge(in_kv[k // 2], 16)
                        split_hi(w_kv[:, 0, k], raw_kv[k // 2][:, k % 2]).then_inc(m["kv_hi"], 1)
                for g in range(4):
                    act.wait_ge(m["z_mm"], 4 * p + g + 1)
                    if p >= 1:
                        act.wait_ge(m["o_mm"], NT * p)
                    h, hf = g // 2, g % 2
                    nc.scalar.copy(zT[:, 0, h, hf * HALF:(hf + 1) * HALF], banks[6 + g % 2][:, 0:HALF])\
                        .then_inc(m["z_hi"], 1)

            def c_high(b):
                act.wait_ge(in_c[b % 2], 16 * (b // 2 + 1))
                if b >= 2:
                    act.wait_ge(m["cv_mm"], CT * (b - 1))
                if b == 1:
                    act.wait_ge(m["o_mm"], NT * NP_)
                split_hi(cT[b % 2][:, 0], raw_c[b % 2]).then_inc(m["c_hi"], 1)

            def std(ln):
                act.wait_ge(m["ve_ok"], ln + 1)
                nc.scalar.activation(ln_sd[:, :], ln_ve[:, :], ACT.Sqrt).then_inc(m["sd_ok"], 1)

            def turned_hi(n, i, bank):
                act.wait_ge(m["t_mm"], i + 1)
                nc.scalar.copy(xT[:, 0, :, n * P:(n + 1) * P],
                               banks[bank][:, :].rearrange("p (k c) -> p k c", k=KC)).then_inc(m["t_hi"], 1)

            def x3_high(j, dst):
                act.wait_ge(in_x3, 16 * (j + 1))
                split_hi(dst[:, 0], raw_x3).then_inc(m["x3_hi"], 1)

            c_high(0)
            c_high(1)
            for n in range(NCT):
                b, c = n // CT, n % CT
                act.wait_ge(m["ck_mm"], n + 1)
                if n >= 2:
                    act.wait_ge(m["phi_ok"], n - 1)
                nc.scalar.activation(relu_c[0:CM, n % 2, :], banks[n % 2][0:CM, :], ACT.Relu).then_inc(m["ck_relu"], 1)
                nc.scalar.activation(exp_c[0:CM, n % 2, :], banks[n % 2][0:CM, :], ACT.Exp).then_inc(m["ck_exp"], 1)
                if c == CT - 1:
                    if b == 0:
                        std(0)
                    if b >= 1:
                        turned_hi(b - 1, b - 1, 7)
                    if b in (1, 3):
                        x3_high(b // 2, (w_q, w_g)[b // 2])
                    if b + 2 < NB:
                        c_high(b + 2)
            for j in range(2 * KC):
                act.wait_ge(m["q2_mm"], j + 1)
                if j >= 2:
                    act.wait_ge(m["q2_phi"], j - 1)
                else:
                    act.wait_ge(m["phi_ok"], NCT)
                nc.scalar.activation(relu_q[:, j % 2, :], banks[j % 2][:, 0:HALF], ACT.Relu)
                nc.scalar.activation(exp_q[:, j % 2, :], banks[j % 2][:, 0:HALF], ACT.Exp).then_inc(m["q2_act"], 1)
            x3_high(2, w_xo)
            act.wait_ge(m["c_lo"], NB)
            for j in range(2 * KC):
                g, hf = j // 2, j % 2
                act.wait_ge(m["g2_mm"], j + 1)
                nc.scalar.activation(sig[:, g, hf * HALF:(hf + 1) * HALF], banks[j % 2][:, 0:HALF], ACT.Sigmoid,
                                     bias=gate_b[:, g:g + 1]).then_inc(m["g2_sig"], 1)
            for b in range(NB):
                act.wait_ge(m["a_gate"], b + 1)
                split_hi(aT[:, 0, :, b * S:(b + 1) * S], atn[:, b % 2]).then_inc(m["a_hi"], 1)
            def gu_high(c, w, k):
                act.wait_ge(in_gu, 16 * c + 16)
                split_hi(w[:, 0, k], raw_gu[:, k]).then_inc(m["gu_hi"], 1)

            std(1)
            for n in range(NT):
                act.wait_ge(m["t_mm"], NT + n + 1)
                if n >= 2:
                    act.wait_ge(m["r_mm"], n - 1)
                nc.scalar.copy(x2T[:, n % 2], banks[4 + n % 2][:, :].rearrange("p (k c) -> p k c", k=KC))\
                    .then_inc(m["x2t_out"], 1)
                split_hi(x_n[:, 0, n], acc[:, n, :]).then_inc(m["n_hi"], 1)
            for k in range(KC):
                gu_high(0, w_gu[0], k)
            act.wait_ge(m["topd_ok"], 1)
            nc.scalar.activation(top_w[:, :, :], top_d[:, :, :], ACT.Sigmoid).then_inc(m["topw_ok"], 1)
            x3_high(3, w_dn)
            act.wait_ge(m["st_mm"], 1)
            nc.scalar.copy(scoreT[0:NE, 0:4 * P], banks[0][0:NE, :]).then_inc(m["st_out"], 1)
            nc.scalar.copy(scoreT[0:NE, 4 * P:T], banks[1][0:NE, 0:T - 4 * P]).then_inc(m["st_out"], 1)

            def gathered_high(c):
                for k in range(KC):
                    act.wait_ge(m["xg_mm"], KC * c + (k + 1))
                    if k == 0 and not (isinstance(c, int) and c == 0):
                        act.wait_ge(m["gu_mm"], KC * c)
                    nc.scalar.copy(x_g[:, 0, k], banks[4 + 2 * (k % 2)][:, 0:CAP]).then_inc(m["xg_hi"], 1)

            def swish(c, q):
                n = KC * c + q
                act.wait_ge(m["gl_ok"], n + 1)
                if not (isinstance(c, int) and n < 2):
                    act.wait_ge(m["pr_ok"], n - 1)
                nc.scalar.activation(sg[:, q % 2], gl[:, q % 2], ACT.Sigmoid, scale=ALPHA).then_inc(m["sg_ok"], 1)

            def h_high(c, q):
                act.wait_ge(m["hh_ok"], KC * c + (q + 1))
                if not (isinstance(c, int) and c == 0):
                    act.wait_ge(m["dn_mm"], 3 * c)
                nc.scalar.copy(hT[:, 0, q], hh[:, q % 2]).then_inc(m["h_hi"], 1)

            def y_evac(c):
                for k in range(3):
                    act.wait_ge(m["dn_mm"], 3 * c + (k + 1))
                    if k == 0 and not (isinstance(c, int) and c == 0):
                        act.wait_ge(y_done, 48 * c)
                    nc.scalar.copy(y[:, k, :], banks[4 + k][:, :]).then_inc(m["y_out"], 1)

            gathered_high(0)
            for e in range(NE):
                for q in range(KC):
                    swish(e, q)
                    if q:
                        h_high(e, q - 1)
                    if q == 1 and e:
                        x3_high(3 + e, w_dn)
                    if e + 1 < NE:
                        if q == 0 and e == 0:
                            act.wait_ge(m["xo_mm"], NT)
                        gu_high(e + 1, w_gu[(e + 1) % 2], q)
                h_high(e, KC - 1)
                if e + 1 < NE:
                    gathered_high(e + 1)
                y_evac(e)
            act.wait_ge(m["more_ok"], 1)
            rounds = act.value_load(more_i[0:1, 0:1], min_val=0, max_val=3)
            with act.If(rounds > 0):
                with act.Fori(0, rounds) as j:
                    with act.Fori(0, NE) as e:
                        c = NE + j * NE + e
                        act.wait_ge(m["gu_mm"], KC * c)
                        act.wait_ge(m["dn_mm"], 3 * c)
                        for k in range(KC):
                            gu_high(c, w_gu[0], k)
                        x3_high(c + 3, w_dn)
                        gathered_high(c)
                        for q in range(KC):
                            swish(c, q)
                            h_high(c, q)
                        y_evac(c)
            std(2)

        @block.vector
        def _(dve):
            def split_lo(dst, src, hi):
                return nc.vector.tensor_tensor(dst, src, bits(hi), ALU.subtract)

            def w_low(p, j):
                dve.wait_ge(m["w_hi"], 3 * p + j + 1)
                split_lo(w_qkv[p % 2][j][:, 1], raw_w[:, j], w_qkv[p % 2][j][:, 0]).then_inc(m["w_lo"], 1)

            def wo_low(p):
                dve.wait_ge(m["wo_hi"], p + 1)
                split_lo(w_o[:, 1], raw_o, w_o[:, 0]).then_inc(m["wo_lo"], 1)

            def v_evac(p, j):
                dve.wait_ge(m["v_mm"], 4 * p + j + 1)
                if p == 0:
                    dve.wait_ge(m["x_lo"], KC)
                if p >= 2:
                    dve.wait_ge(m["z_mm"], 4 * (p - 1))
                nc.vector.tensor_copy(V[0:S, p % 2, 2 * j:2 * j + 2, :],
                                      banks[(1 + j) % 2][0:S, :].rearrange("p (a c) -> p a c", a=2))\
                    .then_inc(m["v_out"], 1)

            def add_out(p):
                for n in range(NT):
                    dve.wait_ge(m["o_mm"], NT * p + n + 1)
                    if p == 0 and n == 0:
                        dve.wait_ge(in_acc, 16)
                    if p >= 1:
                        dve.wait_ge(m["o_add"], NT * (p - 1) + n + 1)
                    nc.vector.tensor_tensor(acc[:, n, :], acc[:, n, :], banks[n % 2][:, :], ALU.add)\
                        .then_inc(m["o_add"], 1)

            for k in range(KC):
                dve.wait_ge(m["x_hi"], k + 1)
                split_lo(xT[:, 1, k], raw_x[:, k], xT[:, 0, k]).then_inc(m["x_lo"], 1)
                if k < 3:
                    w_low(0, k)
            wo_low(0)
            for j in range(3):
                w_low(1, j)
            for j in range(4):
                v_evac(0, j)
            dve.wait_ge(in_const, 16 * 8)
            for p in range(NP_):
                for g in range(4):
                    n = 4 * p + g
                    dve.wait_ge(m["s_mm"], n + 1)
                    if p >= 1:
                        dve.wait_ge(m["pt_mm"], n - 3)
                        dve.wait_ge(m["exp_ok"], n - 3)
                    sc = banks[2 + g % 2][0:S, 0:HALF].rearrange("p (a c) -> p a c", a=BH)
                    nc.vector.scalar_tensor_tensor(prob[0:S, g], sc, -SCALE,
                                                   causal[0:S, :].unsqueeze(1).to_broadcast([S, BH, S]),
                                                   ALU.mult, ALU.subtract).then_inc(m["masked"], 1)
                    dve.wait_ge(m["masked"], n + 1)
                    nc.vector.tensor_reduce(neg_max[0:S, g * BH:(g + 1) * BH], prob[0:S, g], AX.X, ALU.min)\
                        .then_inc(m["neg_max_ok"], 1)
                if p >= 1:
                    add_out(p - 1)
                    wo_low(p)
                dve.wait_ge(m["exp_ok"], 4 * p + 4)
                if p >= 1:
                    dve.wait_ge(m["prob_ok"], 4 * p)
                nc.vector.reciprocal(exp_inv[0:S, :], exp_sum[0:S, :]).then_inc(m["inv_ok"], 1)
                dve.wait_ge(m["inv_ok"], p + 1)
                for g in range(4):
                    nc.vector.tensor_tensor(prob[0:S, g], prob[0:S, g],
                                            exp_inv[0:S, g * BH:(g + 1) * BH].unsqueeze(2).to_broadcast([S, BH, S]),
                                            ALU.mult).then_inc(m["prob_ok"], 1)
                if p + 2 < NP_:
                    for j in range(3):
                        w_low(p + 2, j)
                if p + 1 == NP_:
                    for k in range(KC):
                        dve.wait_ge(m["kv_hi"], k + 1)
                        split_lo(w_kv[:, 1, k], raw_kv[k // 2][:, k % 2], w_kv[:, 0, k]).then_inc(m["kv_lo"], 1)

                def pt(g):
                    n = 4 * p + g
                    dve.wait_ge(m["pt_mm"], n + 1)
                    if n >= 2:
                        dve.wait_ge(m["z_mm"], n - 1)
                    nc.vector.tensor_copy(probT[0:S, g % 2], banks[4 + g % 2][0:S, 0:HALF]
                                          .rearrange("p (a c) -> p a c", a=BH)).then_inc(m["pt_out"], 1)

                def z(g):
                    n, h, hf = 4 * p + g, g // 2, g % 2
                    dve.wait_ge(m["z_hi"], n + 1)
                    split_lo(zT[:, 1, h, hf * HALF:(hf + 1) * HALF], banks[6 + g % 2][:, 0:HALF],
                             zT[:, 0, h, hf * HALF:(hf + 1) * HALF]).then_inc(m["z_lo"], 1)

                pt(0)
                pt(1)
                for g in range(4):
                    if p + 1 < NP_:
                        v_evac(p + 1, g)
                    z(g)
                    if g < 2:
                        pt(g + 2)
            add_out(NP_ - 1)

            def c_low(b):
                dve.wait_ge(m["c_hi"], b + 1)
                split_lo(cT[b % 2][:, 1], raw_c[b % 2], cT[b % 2][:, 0]).then_inc(m["c_lo"], 1)

            def stats(n, ln, added):
                dve.wait_ge(*added)
                if ln:
                    dve.wait_ge(m["mv_ok"], NT * (ln - 1) + n + 1)
                nc.vector.bn_stats(ln_st[:, n, :], acc[:, n, :]).then_inc(m["bn_ok"], 1)

            def normalise(ln):
                for n in range(NT):
                    dve.wait_ge(m["bn_ok"], NT * ln + n + 1)
                    if ln:
                        dve.wait_ge(m["ln_ok"], NT * ln)
                    nc.vector.bn_aggr(ln_mv[:, n, :], ln_st[:, n, :]).then_inc(m["mv_ok"], 1)
                dve.wait_ge(m["mv_ok"], NT * (ln + 1))
                if ln:
                    dve.wait_ge(m["sd_ok"], ln)
                nc.vector.tensor_scalar(ln_ve[:, :], ln_mv[:, :, 1], LN_EPS, None, ALU.add).then_inc(m["ve_ok"], 1)
                dve.wait_ge(m["sd_ok"], ln + 1)
                nc.vector.reciprocal(ln_rs[:, :], ln_sd[:, :]).then_inc(m["rs_ok"], 1)
                dve.wait_ge(m["rs_ok"], ln + 1)
                for n in range(NT):
                    nc.vector.tensor_scalar(acc[:, n, :], acc[:, n, :], ln_mv[:, n, 0:1], ln_rs[:, n:n + 1],
                                            ALU.subtract, ALU.mult).then_inc(m["ln_ok"], 1)

            def turned_lo(n, i, bank):
                dve.wait_ge(m["t_hi"], i + 1)
                split_lo(xT[:, 1, :, n * P:(n + 1) * P], banks[bank][:, :].rearrange("p (k c) -> p k c", k=KC),
                         xT[:, 0, :, n * P:(n + 1) * P]).then_inc(m["t_lo"], 1)

            def x3_low(j, dst):
                dve.wait_ge(m["x3_hi"], j + 1)
                split_lo(dst[:, 1], raw_x3, dst[:, 0]).then_inc(m["x3_lo"], 1)

            def sums_out(b):
                for i in range(2):
                    both = banks[4 + i][:, 0:2 * (P + 1)].rearrange("p (g c) -> p g c", g=2)
                    nc.vector.tensor_tensor(kv_sum[:, b, 2 * i:2 * i + 2], both[:, :, 0:P],
                                            blocks[:, :].unsqueeze(1).to_broadcast([P, 2, P]), ALU.mult)\
                        .then_inc(m["sum_out"], 1)
                    nc.vector.tensor_copy(k_sum[:, b, 2 * i:2 * i + 2].unsqueeze(2), both[:, :, P:P + 1])\
                        .then_inc(m["sum_out"], 1)

            dve.wait_ge(m["s_mm"], 4 * NP_)
            nc.vector.memset(v_c[:, :, :, P:P + 2], 1.0).then_inc(m["ones_col"], 1)
            c_low(0)
            c_low(1)
            for n in range(NCT):
                b, c = n // CT, n % CT
                dve.wait_ge(m["ck_exp"], n + 1)
                if n >= 3:
                    dve.wait_ge(m["sum_mm"], n - 2)
                nc.vector.scalar_tensor_tensor(phi_k[0:CM, n % 3, :], exp_c[0:CM, n % 2, :], 1.0,
                                               relu_c[0:CM, n % 2, :], ALU.min, ALU.add).then_inc(m["phi_ok"], 1)
                dve.wait_ge(m["cv_mm"], n + 1)
                nc.vector.tensor_copy(v_c[0:CM, n % 3, :, 0:P], banks[2 + n % 2][0:CM, :]
                                      .rearrange("p (k c) -> p k c", k=KC)).then_inc(m["cv_out"], 1)
                if c == 0 and b >= 1:
                    dve.wait_ge(m["sum_mm"], CT * b)
                    sums_out(b - 1)
                if c == CT - 1:
                    if b == 0:
                        for j in range(NT):
                            stats(j, 0, (m["o_add"], NT * (NP_ - 1) + j + 1))
                        normalise(0)
                        nc.vector.tensor_scalar(gu_b[:, :, KC:2 * KC], gu_b[:, :, KC:2 * KC], 1.0, None, ALU.add)\
                            .then_inc(m["gub_ok"], 1)
                    if b >= 1:
                        turned_lo(b - 1, b - 1, 7)
                    if b in (1, 3):
                        x3_low(b // 2, (w_q, w_g)[b // 2])
                    if b + 2 < NB:
                        c_low(b + 2)
            b = NB
            dve.wait_ge(m["sum_mm"], CT * b)
            sums_out(b - 1)

            for j in range(2 * KC):
                g, hf = j // 2, j % 2
                dve.wait_ge(m["q2_act"], j + 1)
                nc.vector.scalar_tensor_tensor(phi_q[:, g, hf * HALF:(hf + 1) * HALF], exp_q[:, j % 2, :], 1.0,
                                               relu_q[:, j % 2, :], ALU.min, ALU.add).then_inc(m["q2_phi"], 1)
            x3_low(2, w_xo)
            for b in range(NB):
                at = atn[:, b % 2]
                den = banks[6 + b % 2][:, 0:HALF].rearrange("p (k c) -> p k c", k=KC)
                num = banks[4 + b % 2][:, 0:HALF].rearrange("p (k c) -> p k c", k=KC)
                dve.wait_ge(m["a_mm"], b + 1)
                if b >= 2:
                    dve.wait_ge(m["a_lo"], b - 1)
                if b == 0:
                    dve.wait_ge(m["q2_phi"], 2 * KC)
                nc.vector.tensor_scalar(at, den, DEN_EPS, None, ALU.add).then_inc(m["a_den"], 1)
                dve.wait_ge(m["a_den"], b + 1)
                nc.vector.reciprocal(at, at).then_inc(m["a_inv"], 1)
                dve.wait_ge(m["a_inv"], b + 1)
                nc.vector.tensor_tensor(at, num, at, ALU.mult).then_inc(m["a_num"], 1)
                dve.wait_ge(m["a_num"], b + 1)
                dve.wait_ge(m["g2_sig"], 2 * KC)
                nc.vector.tensor_tensor(at, at, sig[:, :, b * S:(b + 1) * S], ALU.mult).then_inc(m["a_gate"], 1)
                dve.wait_ge(m["a_hi"], b + 1)
                split_lo(aT[:, 1, :, b * S:(b + 1) * S], at, aT[:, 0, :, b * S:(b + 1) * S]).then_inc(m["a_lo"], 1)

            def gu_low(e, k):
                dve.wait_ge(m["gu_hi"], KC * e + k + 1)
                split_lo(w_gu[e % 2][:, 1, k], raw_gu[:, k], w_gu[e % 2][:, 0, k]).then_inc(m["gu_lo"], 1)

            for n in range(NT):
                dve.wait_ge(m["xo_mm"], n + 1)
                dve.wait_ge(m["ln_ok"], n + 1)
                nc.vector.tensor_tensor(acc[:, n, :], acc[:, n, :], banks[2 + n % 2][:, :], ALU.add)\
                    .then_inc(m["xo_add"], 1)
            for n in range(NT):
                stats(n, 1, (m["xo_add"], n + 1))
            normalise(1)
            for n in range(NT):
                dve.wait_ge(m["n_hi"], n + 1)
                split_lo(x_n[:, 1, n], acc[:, n, :], x_n[:, 0, n]).then_inc(m["n_lo"], 1)
            dve.wait_ge(m["r_mm"], NT)
            nc.vector.tensor_tensor(logit[:, :, :], banks[6][:, 0:NT * NE].rearrange("p (n e) -> p n e", n=NT),
                                    rt_b[:, :].unsqueeze(1).to_broadcast([P, NT, NE]), ALU.add)\
                .then_inc(m["log_ok"], 1)
            dve.wait_ge(m["log_ok"], 1)
            for n in range(NT):
                nc.vector.max(top[:, n, :], logit[:, n, :]).then_inc(m["top_ok"], 1)
            for n in range(NT):
                dve.wait_ge(m["top_ok"], n + 1)
                nc.vector.max_index(top_i[:, n, :], top[:, n, :], logit[:, n, :]).then_inc(m["idx_ok"], 1)
            nc.vector.tensor_tensor(top_d[:, :, 0:1], top[:, :, 0:1], top[:, :, 1:2], ALU.subtract)
            nc.vector.tensor_tensor(top_d[:, :, 1:2], top[:, :, 1:2], top[:, :, 0:1], ALU.subtract)\
                .then_inc(m["topd_ok"], 1)
            dve.wait_ge(m["idx_ok"], NT)
            nc.vector.tensor_copy(top_f[:, :, :], top_i[:, :, 0:2]).then_inc(m["topf_ok"], 1)
            dve.wait_ge(m["topf_ok"], 1)
            every = [P, NT, NE]
            for j in range(2):
                nc.vector.tensor_tensor(hot[:, j], iota[:, :].unsqueeze(1).to_broadcast(every),
                                        top_f[:, :, j:j + 1].to_broadcast(every), ALU.is_equal)\
                    .then_inc(m["hot_ok"], 1)
            dve.wait_ge(m["hot_ok"], 2)
            nc.vector.tensor_tensor(chosen[:, :, :], hot[:, 0], hot[:, 1], ALU.add).then_inc(m["chosen_ok"], 1)
            dve.wait_ge(m["topw_ok"], 1)
            for j in range(2):
                nc.vector.tensor_tensor(pick[:, j], hot[:, j], top_w[:, :, j:j + 1].to_broadcast(every),
                                        ALU.mult).then_inc(m["pick_ok"], 1)
            dve.wait_ge(m["pick_ok"], 2)
            nc.vector.tensor_tensor(score[:, :, :], pick[:, 0], pick[:, 1], ALU.add).then_inc(m["score_ok"], 1)
            dve.wait_ge(m["rank_mm"], 1)
            nc.vector.tensor_copy(rank[:, :, :], banks[7][:, 0:NT * NE].rearrange("p (n e) -> p n e", n=NT))\
                .then_inc(m["rank_ok"], 1)
            nc.vector.tensor_reduce(most[:, 0:1], banks[7][:, NT * NE:(NT + 1) * NE], AX.X, ALU.max)\
                .then_inc(m["rank_ok"], 1)
            dve.wait_ge(m["rank_ok"], 2)
            nc.vector.scalar_tensor_tensor(slot_of[:, 0].rearrange("p e n -> p n e"), rank[:, :, :], 1.0,
                                           chosen[:, :, :], ALU.add, ALU.mult).then_inc(m["slot_ok"], 1)
            dve.wait_ge(m["slot_ok"], 1)
            nc.vector.tensor_scalar(slot_of[:, 0], slot_of[:, 0], -1.0, None, ALU.add).then_inc(m["slot_ok"], 1)
            dve.wait_ge(m["slot_ok"], 2)
            for j in range(3):
                nc.vector.tensor_scalar(slot_of[:, j + 1], slot_of[:, 0], -float((j + 1) * CAP), None, ALU.add)\
                    .then_inc(m["slot_ok"], 1)
            for j in range(3):
                nc.vector.tensor_scalar(most[:, j + 1:j + 2], most[:, 0:1], float((j + 1) * CAP), None, ALU.is_gt)\
                    .then_inc(m["level_ok"], 1)
            dve.wait_ge(m["level_ok"], 3)
            nc.vector.tensor_reduce(most[:, 4:5], most[:, 1:4], AX.X, ALU.add).then_inc(m["level_ok"], 1)
            for j in range(2):
                nc.vector.tensor_tensor(hot[:, j], hot[:, j], rank[:, :, :], ALU.mult).then_inc(m["level_ok"], 1)
            dve.wait_ge(m["level_ok"], 4)
            nc.vector.tensor_copy(more_i[:, :], most[:, 4:5]).then_inc(m["more_ok"], 1)
            for j in range(2):
                dve.wait_ge(m["level_ok"], 5 + j)
                nc.vector.tensor_reduce(pick_slot[:, :, j:j + 1], hot[:, j], AX.X, ALU.add).then_inc(m["level_ok"], 1)

            def rows_of(r):
                if isinstance(r, int):
                    dve.wait_ge(m["level_ok"], 8)
                else:
                    dve.wait_ge(m["now_slot"], r)
                nc.vector.tensor_scalar(near[:, :, :], pick_slot[:, :, :], 0.0, float(CAP - 1), ALU.max, ALU.min)\
                    .then_inc(m["near_ok"], 1)
                nc.vector.tensor_scalar(here[:, :, :], pick_slot[:, :, :], float(CAP), None, ALU.is_lt)\
                    .then_inc(m["here_ok"], 1)
                dve.wait_ge(m["near_ok"], 2 * r + 1)
                nc.vector.scalar_tensor_tensor(near[:, :, :], top_f[:, :, :], float(CAP), near[:, :, :],
                                               ALU.mult, ALU.add).then_inc(m["near_ok"], 1)
                dve.wait_ge(m["here_ok"], 2 * r + 1)
                nc.vector.scalar_tensor_tensor(here[:, :, :], pick_slot[:, :, :], 0.0, here[:, :, :],
                                               ALU.is_ge, ALU.mult).then_inc(m["here_ok"], 1)
                dve.wait_ge(m["near_ok"], 2 * r + 2)
                nc.vector.tensor_copy(y_row[:, :, :], near[:, :, :]).then_inc(m["row_ok"], 1)
                dve.wait_ge(m["here_ok"], 2 * r + 2)
                nc.vector.tensor_tensor(w_now[:, :, :], here[:, :, :], top_w[:, :, :], ALU.mult)\
                    .then_inc(m["w_ok"], 1)
                nc.vector.tensor_scalar(pick_slot[:, :, :], pick_slot[:, :, :], -float(CAP), None, ALU.add)\
                    .then_inc(m["now_slot"], 1)

            def combine(r, uses):
                dve.wait_ge(m["w_ok"], r + 1)
                for i in range(2 * NT):
                    n, j = i // 2, i % 2
                    dve.wait_ge(y_in[i % 8], uses(i))
                    dve.wait_ge(m["comb"], r * (2 * NT) + i) if not (isinstance(r, int) and i == 0) else None
                    nc.vector.scalar_tensor_tensor(acc[:, n, :], y_got[:, i % 8, :], w_now[:, n, j:j + 1],
                                                   acc[:, n, :], ALU.mult, ALU.add).then_inc(m["comb"], 1)

            rows_of(0)
            for k in range(KC):
                gu_low(0, k)
            x3_low(3, w_dn)

            def gathered_low(c):
                for k in range(KC):
                    dve.wait_ge(m["xg_mm"], KC * c + (k + 1))
                    if k == 0 and not (isinstance(c, int) and c == 0):
                        dve.wait_ge(m["gu_mm"], KC * c)
                    nc.vector.tensor_copy(x_g[:, 1, k], banks[5 + 2 * (k % 2)][:, 0:CAP]).then_inc(m["xg_lo"], 1)

            def h_low(c, q):
                dve.wait_ge(m["h_hi"], KC * c + (q + 1))
                split_lo(hT[:, 1, q], hh[:, q % 2], hT[:, 0, q]).then_inc(m["h_lo"], 1)

            def clamp(c, q, bias):
                n = KC * c + q
                later = not (isinstance(c, int) and n < 2)
                dve.wait_ge(m["gu_mm"], n + 1)
                if later:
                    dve.wait_ge(m["pr_ok"], n - 1)
                nc.vector.tensor_scalar(gl[:, q % 2], banks[q % 2][:, 0:CAP], bias[:, q:q + 1], LIMIT,
                                        ALU.add, ALU.min).then_inc(m["gl_ok"], 1)
                if later:
                    dve.wait_ge(m["hh_ok"], n - 1)
                nc.vector.tensor_scalar(up[:, q % 2], banks[2 + q % 2][:, 0:CAP], bias[:, KC + q:KC + q + 1],
                                        LIMIT + 1, ALU.add, ALU.min).then_inc(m["up_ok"], 1)

            def hidden(c, q):
                n = KC * c + q
                dve.wait_ge(m["pr_ok"], n + 1)
                dve.wait_ge(m["up_ok"], n + 1)
                if not (isinstance(c, int) and n < 2):
                    dve.wait_ge(m["h_lo"], n - 1)
                nc.vector.scalar_tensor_tensor(hh[:, q % 2], up[:, q % 2], 1 - LIMIT, pr[:, q % 2],
                                               ALU.max, ALU.mult).then_inc(m["hh_ok"], 1)

            for n in range(NT):
                dve.wait_ge(m["db_mm"], n + 1)
                dve.wait_ge(m["n_lo"], NT)
                nc.vector.tensor_tensor(acc[:, n, :], acc[:, n, :], banks[2 + n % 2][:, :], ALU.add)\
                    .then_inc(m["db_add"], 1)
            gathered_low(0)
            dve.wait_ge(m["gub_ok"], 1)
            for e in range(NE):
                for q in range(KC):
                    clamp(e, q, gu_b[:, e])
                    if q:
                        hidden(e, q - 1)
                        h_low(e, q - 1)
                    if q in (1, 2) and e + 1 < NE:
                        gu_low(e + 1, q - 1)
                    if q == 3 and e:
                        x3_low(3 + e, w_dn)
                hidden(e, KC - 1)
                h_low(e, KC - 1)
                if e + 1 < NE:
                    gathered_low(e + 1)
                    gu_low(e + 1, 2)
                    gu_low(e + 1, 3)
            dve.wait_ge(m["db_add"], NT)
            combine(0, lambda i: 16 * (i // 8 + 1))
            rounds = dve.value_load(more_i[0:1, 0:1], min_val=0, max_val=3)
            with dve.If(rounds > 0):
                with dve.Fori(0, rounds) as j:
                    with dve.Fori(0, NE) as e:
                        c = NE + j * NE + e
                        for k in range(KC):
                            dve.wait_ge(m["gu_hi"], KC * c + (k + 1))
                            split_lo(w_gu[0][:, 1, k], raw_gu[:, k], w_gu[0][:, 0, k]).then_inc(m["gu_lo"], 1)
                        x3_low(c + 3, w_dn)
                        dve.wait_ge(in_more, (j * NE + e) * 32 + 32)
                        nc.vector.tensor_scalar(more_b[:, KC:2 * KC], more_b[:, KC:2 * KC], 1.0, None, ALU.add)\
                            .then_inc(m["moreb_ok"], 1)
                        dve.wait_ge(m["moreb_ok"], (j * NE + e) + 1)
                        gathered_low(c)
                        for q in range(KC):
                            clamp(c, q, more_b)
                            hidden(c, q)
                            h_low(c, q)
                    rows_of(j + 1)
                    combine(j + 1, lambda i: j * (32 if i % 8 < 6 else 16) + (32 if i % 8 < 6 else 16) + 16 * (i // 8 + 1))
                    dve.drain()
            for n in range(NT):
                stats(n, 2, (m["comb"], 2 * NT))
            normalise(2)


def kernel(x, ctx_2048, L0_attn_W_Q, L0_attn_W_K, L0_attn_W_V, L0_attn_W_O, L0_xattn_Wq, L0_xattn_Wg, L0_xattn_bg,
           L0_xattn_Wkv, L0_xattn_Wo, L0_ffn_router_weight, L0_ffn_router_bias, L0_ffn_gate_up_proj,
           L0_ffn_gate_up_proj_bias, L0_ffn_down_proj, L0_ffn_down_proj_bias):
    import numpy as np
    import concourse.bacc as _bacc
    from concourse.bass_utils import run_bass_kernel_spmd as _run

    def arr(a):
        return np.asarray(a)

    NB, S, D = x.shape
    T, KC = NB * S, D // P
    H = L0_attn_W_Q.shape[0]

    def cols(w, parts=KC):
        return arr(w).T.reshape(parts, P, -1).transpose(1, 0, 2)

    def pairs(w):
        return arr(w).reshape(H // 2, 2 * P, KC, P).transpose(0, 3, 2, 1)

    gu = arr(L0_ffn_gate_up_proj)
    NE = gu.shape[0]
    gub = arr(L0_ffn_gate_up_proj_bias).reshape(NE, D, 2)
    causal = np.where(np.arange(S)[None, :] > np.arange(P)[:, None], np.float32(NEG), np.float32(0))
    blocks = (np.arange(P)[:, None] // 32 == np.arange(P)[None, :] // 32).astype(np.float32)
    arrays = {
        "x": arr(x),
        "x_t": cols(arr(x).reshape(T, D)),
        "w_qkv": np.stack([pairs(L0_attn_W_Q), pairs(L0_attn_W_K), pairs(L0_attn_W_V)], 2),
        "w_o": arr(L0_attn_W_O).reshape(H // 2, 2, D, P).transpose(0, 3, 1, 2),
        "ctx_t": arr(ctx_2048).transpose(0, 2, 1).reshape(NB, KC, P, -1).transpose(0, 2, 1, 3),
        "w_kv": cols(L0_xattn_Wkv),
        "w_x3": np.stack([cols(L0_xattn_Wq), cols(L0_xattn_Wg), cols(L0_xattn_Wo)]),
        "gate_b": arr(L0_xattn_bg).reshape(KC, P).T,
        "rt_w": cols(L0_ffn_router_weight),
        "rt_b": np.broadcast_to(arr(L0_ffn_router_bias), (P, NE)),
        "w_gu": np.concatenate([gu[:, :, 0::2], gu[:, :, 1::2]], 2).reshape(NE, KC, P, -1).transpose(0, 2, 1, 3),
        "gu_b": np.concatenate([gub[:, :, 0].reshape(NE, KC, P), gub[:, :, 1].reshape(NE, KC, P)], 1).transpose(2, 0, 1),
        "w_down": arr(L0_ffn_down_proj).reshape(NE, KC, P, D).transpose(0, 2, 1, 3),
        "dn_b": arr(L0_ffn_down_proj_bias),
        "ident": np.eye(P, dtype=np.float32),
        "causal": causal,
        "blocks": blocks,
        "iota_c": np.broadcast_to(np.arange(CAP, dtype=np.float32), (P, CAP)),
        "before": np.triu(np.ones((P, P), np.float32), 1),
        "all_ones": np.ones((P, P), np.float32),
        "iota": np.broadcast_to(np.arange(NE, dtype=np.float32), (P, NE)),
    }
    nc = _bacc.Bacc("TRN2", target_bir_lowering=False, num_devices=1)
    feed, args = {}, {}
    for name, a in arrays.items():
        a = np.ascontiguousarray(a)
        feed[f"in_{name}_dram"] = a
        args[name] = nc.dram_tensor(f"in_{name}_dram", a.shape, mybir.dt.from_np(a.dtype), kind="ExternalInput").ap()
    out = nc.dram_tensor("out_0_dram", (NB, S, D), F32, kind="ExternalOutput").ap()
    decoder_layer(nc, args, out)
    res = _run(nc, [feed], core_ids=[0])
    return res.results[0]["out_0_dram"]
```
